# Optimizing a Trainium2 kernel written in Bass

```python
import numpy as np
import jax
import jax.numpy as jnp

def _softmax(x, axis=-1):
    return jax.nn.softmax(x, axis=axis)

def _gelu(x):
    return jax.nn.gelu(x, approximate=True)

def _silu(x):
    return jax.nn.silu(x)

def _sigmoid(x):
    return jax.nn.sigmoid(x)

def _layernorm(x, axis=-1, eps=1e-05):
    m = jnp.mean(x, axis=axis, keepdims=True)
    v = jnp.var(x, axis=axis, keepdims=True)
    return (x - m) / jnp.sqrt(v + eps)

def _scatter_add(tgt, idx, src, axis=0):
    return tgt.at[idx].add(src)

def _segment_sum(src, seg, n):
    return jax.ops.segment_sum(src, seg, n)
kernel_name = 'mk_gnn_preln_d1_gnn_r8_da53ee'

def setup_inputs(seed: int=0):
    np.random.seed(seed)
    _w = jnp.asarray

    def _rec_inputs():
        import jax
        import jax.numpy as jnp
        _gk = jax.random.key(seed)
        x = -0.000202 + 1 * jax.random.normal(jax.random.fold_in(_gk, 1), (6250, 128), jnp.float32)
        src = jax.random.randint(jax.random.fold_in(_gk, 2), (200000,), 0, 6250, jnp.int32)
        dst = jnp.minimum((6250 * jax.random.uniform(jax.random.fold_in(_gk, 3), (200000,)) ** 2.0).astype(jnp.int32), 49999)
        _o = jnp.argsort(dst, stable=True)
        src = src[_o]
        dst = dst[_o]
        return (x, src, dst)
    x, src, dst = _rec_inputs()

    def _L0_gnn_setup():
        import jax, jax.numpy as jnp
        import numpy as np
        N_NODES = 6250
        N_EDGES = 50000
        IN_DIM = 128
        HIDDEN = 128
        OUT_DIM = 128
        MIX = 4

        def _gelu(x):
            return jax.nn.gelu(x, approximate=False)
        key = jax.random.key(seed)
        ks = jax.random.split(key, 8)
        X = jax.random.normal(ks[0], (N_NODES, IN_DIM), dtype=jnp.float32)
        edge_index = jax.random.randint(ks[1], (2, N_EDGES), 0, N_NODES, dtype=jnp.int64)
        s = lambda fan_in: 1.0 / np.sqrt(fan_in)
        W1 = jax.random.uniform(ks[2], (HIDDEN, IN_DIM), jnp.float32, -s(IN_DIM), s(IN_DIM))
        b1 = jax.random.uniform(ks[3], (HIDDEN,), jnp.float32, -s(IN_DIM), s(IN_DIM))
        WA = jax.random.uniform(ks[4], (HIDDEN, HIDDEN), jnp.float32, -s(HIDDEN), s(HIDDEN))
        WB = jax.random.uniform(ks[5], (MIX, HIDDEN), jnp.float32, -s(HIDDEN), s(HIDDEN))
        W2 = jax.random.uniform(ks[6], (OUT_DIM, 2 * HIDDEN), jnp.float32, -s(2 * HIDDEN), s(2 * HIDDEN))
        b2 = jax.random.uniform(ks[7], (OUT_DIM,), jnp.float32, -s(2 * HIDDEN), s(2 * HIDDEN))
        return {'X': X, 'edge_index': edge_index, 'W1': W1, 'b1': b1, 'WA': WA, 'WB': WB, 'W2': W2, 'b2': b2}
    _L0_gnn_all = _L0_gnn_setup()
    _L0_gnn_in = {k: v for k, v in _L0_gnn_all.items() if k in ('W1', 'b1', 'WA', 'WB', 'W2', 'b2')}
    del _L0_gnn_all
    return {'x': x, 'src': src, 'dst': dst, 'L0_gnn_W1': _L0_gnn_in['W1'], 'L0_gnn_b1': _L0_gnn_in['b1'], 'L0_gnn_WA': _L0_gnn_in['WA'], 'L0_gnn_WB': _L0_gnn_in['WB'], 'L0_gnn_W2': _L0_gnn_in['W2'], 'L0_gnn_b2': _L0_gnn_in['b2']}

def reference(x, src, dst, L0_gnn_W1, L0_gnn_b1, L0_gnn_WA, L0_gnn_WB, L0_gnn_W2, L0_gnn_b2):
    import jax
    import jax.numpy as jnp

    def _L0_gnn_ref(X, edge_index, W1, b1, WA, WB, W2, b2):
        import jax, jax.numpy as jnp
        import numpy as np
        N_NODES = 6250
        N_EDGES = 50000
        IN_DIM = 128
        HIDDEN = 128
        OUT_DIM = 128
        MIX = 4

        def _gelu(x):
            return jax.nn.gelu(x, approximate=False)
        num_nodes = X.shape[0]
        H = _gelu(X @ W1.T + b1)
        src, dst = (edge_index[0], edge_index[1])
        X_src = H[src]
        W_tar = _gelu(X_src @ WA.T) @ WB.T
        cross = X_src[:, :, None] * W_tar[:, None, :]
        agg = jax.ops.segment_sum(cross, dst, num_segments=num_nodes)
        agg = _gelu(agg)
        out_edge = jnp.einsum('ehm,em->eh', agg[dst], W_tar)
        ones = jnp.ones((src.shape[0],), X.dtype)
        cnt = jax.ops.segment_sum(ones, dst, num_segments=num_nodes)
        agg_node = jax.ops.segment_sum(out_edge, dst, num_segments=num_nodes)
        agg_node = agg_node / jnp.maximum(cnt, 1.0)[:, None]
        feat = _gelu(jnp.concatenate([agg_node, H], axis=1))
        out = feat @ W2.T + b2
        return out
    edge_index = jnp.stack([src, dst])
    h = jnp.maximum(_layernorm(x, axis=-1), 0.0)
    x = x + _L0_gnn_ref(h, edge_index, L0_gnn_W1, L0_gnn_b1, L0_gnn_WA, L0_gnn_WB, L0_gnn_W2, L0_gnn_b2)
    return x

_drawn_inputs = setup_inputs


def setup_inputs(seed=0):
    import zlib

    import numpy as np

    out = dict(_drawn_inputs(seed))
    spreads = {}
    factors = {'L0_gnn_b1': 6.811, 'L0_gnn_WA': 8.0, 'L0_gnn_WB': 8.0}
    for name, (base, spread) in spreads.items():
        noise = np.random.default_rng([zlib.crc32(name.encode()), seed]).standard_normal(out[name].shape)
        drawn = base * np.exp(spread * noise) if base else spread * noise
        out[name] = jnp.asarray(drawn.astype(out[name].dtype))
    for name, factor in factors.items():
        out[name] = (out[name] * factor).astype(out[name].dtype)
    return out
```

```python
import concourse.bass as bass
from concourse import mybir
from contextlib import ExitStack

P = 128
N = 6250
E = 200000
D = 128
MIX = 4
NT = -(-N // P)
NCH = -(-NT // 4)
G = 2
HALF = 8
U = 2 * HALF
GPH = HALF // G
GPS = U // G
STEPS = -(-E // (P * U))
ET = STEPS * U
NG = ET // G
GP = 112
GC = NG // GP
W = 24
PASSES = -(-N // W)
NACC = N + W
MS = 3
ROW = D + MIX
RS = ROW + MIX
PAD_DST = 1 << 20
EPS = 1e-5
RSQRT_BITS = 0x5F3759DF
assert NG == GP * GC and NACC >= NT * P


def gnn_kernel(nc, x, src_e, dst_e, dst_g, w1t, b1, wat, wbt, w2t, b2, out):
    f32 = mybir.dt.float32
    i32 = mybir.dt.int32
    ALU = mybir.AluOpType
    ACT = mybir.ActivationFunctionType
    AX = mybir.AxisListType

    ctx = ExitStack()
    with ctx:
        def sb(name, shape, dt=f32):
            return ctx.enter_context(nc.sbuf_tensor(name, shape, dt))

        def sem(name):
            return ctx.enter_context(nc.semaphore(name))

        table = nc.dram_tensor("node_table", [NT * P, ROW], f32, kind="Internal").ap()
        bounds = nc.dram_tensor("window_bounds", [2, NG], i32, kind="Internal").ap()

        x_sb = sb("x_sb", [P, NT, D])
        ht = sb("ht", [P, 2, 4 * P])
        gh = sb("gh", [P, 4 * P])
        acc = sb("acc", [P, MIX, NACC])
        accs = sb("accs", [2 * MIX, NACC])
        src_i = sb("src_i", [P, ET], i32)
        dst_i = sb("dst_i", [P, ET], i32)
        dloc = dst_i[:, :].bitcast(f32)
        gmin = sb("gmin", [GP, GC], i32)
        gmax = sb("gmax", [GP, GC], i32)
        gspan = sb("gspan", [GP, GC], i32)
        base = sb("base", [P, NG], i32)
        span = sb("span", [1, 1], i32)
        idx = sb("idx", [P, 2, HALF], i32)
        ring = sb("ring", [P, U, RS])
        mask = sb("mask", [P, MS, G, MIX + 1, W])
        iota = sb("iota", [P, MIX + 1, W])
        ident = sb("ident", [P, P])
        w1_sb = sb("w1_sb", [P, D])
        wa_sb = sb("wa_sb", [P, D])
        wb_sb = sb("wb_sb", [P, MIX])
        w2_sb = sb("w2_sb", [P, 2, D])
        b1_sb = sb("b1_sb", [P, 1])
        b2_sb = sb("b2_sb", [P, D])
        sel = sb("sel", [MIX, MIX, P])
        down = sb("down", [2 * MIX, MIX])
        stats = sb("stats", [P, NT, 6])
        mv = sb("mv", [P, NT, 2])
        rstd = sb("rstd", [P, NT])
        newton = sb("newton", [P, NT])
        res = sb("res", [P, 2, 4, D])
        z = res[:, 0, :, :]
        hn = res[:, 1, :, :].rearrange("p a d -> p (a d)")
        fa = sb("fa", [P, 4 * P])
        gu = fa
        row = sb("row", [P, 2, 4, ROW])
        sp = row[0:MIX, 0, :, :].rearrange("p a d -> p (a d)")
        prod = sb("prod", [P, MIX, 4 * P])
        dstg = prod[0:GP, :, :].bitcast(i32).rearrange("p m n -> p (m n)")[:, 0:GC * G * P]\
            .rearrange("p (c e) -> p c e", c=GC)
        spans = prod[0:1, 0:2, :].bitcast(i32).rearrange("p m n -> p (m n)")[:, 0:NG]

        ps = ctx.enter_context(nc.psum_tensor("ps", [P, 8, 512], f32))

        ld_x = [sem(f"ld_x{i}") for i in range(4)]
        ld_w = sem("ld_w")
        ld_b2 = sem("ld_b2")
        ld_src = sem("ld_src")
        ld_dst = sem("ld_dst")
        ld_dstg = sem("ld_dstg")
        consts = sem("consts")
        zeroed = sem("zeroed")
        dve = sem("dve_chain")
        st_bounds = sem("st_bounds")
        ld_base = sem("ld_base")
        base_ready = sem("base_ready")
        bounds_ready = sem("bounds_ready")
        z_ready = sem("z_ready")
        zt_ready = sem("zt_ready")
        hn_ready = sem("hn_ready")
        h_ready = sem("h_ready")
        ht_ready = sem("ht_ready")
        u_ready = sem("u_ready")
        gu_ready = sem("gu_ready")
        rows_ready = sem("rows_ready")
        row_copied = sem("row_copied")
        row_stored = [sem(f"row_stored{i}") for i in range(2)]
        idx_ready = sem("idx_ready")
        gathered = [sem(f"gathered{i}") for i in range(U)]
        masks_ready = sem("masks_ready")
        group_summed = sem("group_summed")
        added = sem("added")
        moved = sem("moved")
        span_ready = sem("span_ready")
        edges_done = sem("edges_done")
        own_ready = sem("own_ready")
        own_added = sem("own_added")
        gh_ready = sem("gh_ready")
        ga_ready = sem("ga_ready")
        counts_ready = sem("counts_ready")
        sp_ready = sem("sp_ready")
        spread = sem("spread")
        prod_ready = sem("prod_ready")
        node_ready = sem("node_ready")
        fa_ready = sem("fa_ready")
        out_ready = sem("out_ready")
        res_ready = sem("res_ready")
        res_stored = [sem(f"res_stored{i}") for i in range(2)]

        block = ctx.enter_context(nc.Block())

        def tiles(c):
            return range(4 * c, min(4 * c + 4, NT))

        def cols(c):
            return slice(512 * c, 512 * c + P * len(tiles(c)))

        XQ = [0, 4, 16, 32, NT]

        def x_part(c):
            return next(q for q in range(4) if 4 * c < XQ[q + 1])

        def gathers(pool, before):
            with pool.Fori(0, STEPS) as i:
                n = before + i
                for h in range(2):
                    pool.wait_ge(idx_ready, 2 * n + h + 1)
                    pool.nop(nofuse=True)
                    for k in range(HALF):
                        s = HALF * h + k
                        pool.indirect_dma_start(
                            out=ring[:, s, 0:ROW], out_offset=None, in_=table,
                            in_offset=bass.IndirectOffsetOnAxis(ap=idx[:, h, k:k + 1], axis=0),
                        ).then_inc(gathered[s], 16)

        def node_gelu(act, c):
            k = P * len(tiles(c))
            act.wait_ge(node_ready, c + 1)
            if c > 0:
                act.wait_ge(out_ready, c)
            nc.scalar.activation(fa[:, 0:k], prod[:, 0, 0:k], ACT.Gelu).then_inc(fa_ready, 1)

        def index_copies(act, before):
            with act.Fori(0, STEPS) as i:
                n = before + i
                for h in range(2):
                    act.wait_ge(group_summed, GPS * n + GPH * (h + 1))
                    nc.scalar.activation(idx[:, h, :], src_i[:, bass.ds(U * i + HALF * h, HALF)],
                                         ACT.Copy).then_inc(idx_ready, 1)

        def results(v, c):
            k = len(tiles(c))
            v.wait_ge(out_ready, c + 1)
            if c == 0:
                v.wait_ge(own_added, NCH)
            if c >= 2:
                v.wait_ge(res_stored[c % 2], 16 * (c // 2))
            nc.vector.tensor_tensor(res[:, c % 2, 0:k, :],
                                    ps[:, 4 + c % 2, 0:P * k].rearrange("p (a d) -> p a d", d=D),
                                    x_sb[:, 4 * c:4 * c + k, :], ALU.add).then_inc(res_ready, 1)

        def table_rows(v, c):
            k = len(tiles(c))
            v.wait_ge(rows_ready, c + 1)
            if c >= 2:
                v.wait_ge(row_stored[c % 2], 16 * (c // 2))
            nc.vector.tensor_copy(row[:, c % 2, 0:k, 0:D],
                                  ps[:, 4 + c % 2, 0:P * k].rearrange("p (a d) -> p a d", d=D))
            nc.vector.tensor_copy(row[:, c % 2, 0:k, D:ROW],
                                  ps[:, 6, 0:MIX * k].rearrange("p (a m) -> p a m", m=MIX))\
                .then_inc(row_copied, 1)
            v.wait_ge(own_ready, c + 1)
            nc.vector.tensor_tensor(x_sb[:, 4 * c:4 * c + k, :], x_sb[:, 4 * c:4 * c + k, :],
                                    ps[:, 7, 0:P * k].rearrange("p (a d) -> p a d", d=D),
                                    ALU.add).then_inc(own_added, 1)

        def scatter(v, before):
            with v.Fori(0, STEPS) as i:
                n = before + i

                def masks(j):
                    for t in range(G):
                        s = G * j + t
                        v.wait_ge(gathered[s], 16 * n + 16)
                        last = nc.vector.scalar_tensor_tensor(
                            mask[:, j % MS, t, :, :], iota[:, :, :], dloc[:, bass.ds(U * i + s, 1)],
                            ring[:, s, D:D + MIX + 1][:, :, None].to_broadcast([P, MIX + 1, W]),
                            ALU.is_equal, ALU.mult)
                    last.then_inc(masks_ready, 1)

                def add(j):
                    start = v.value_load(base[0:1, bass.ds(GPS * i + j, 1)], min_val=0, max_val=N)
                    v.wait_ge(group_summed, GPS * n + GPS + j + 1)
                    v.wait_ge(added, 2 * (GPS * n + j) + 1)
                    at = acc[:, :, bass.ds(start, W)]
                    nc.vector.tensor_tensor(at, at, ps[:, j % MS, 0:MIX * W].rearrange("p (m w) -> p m w", w=W),
                                            ALU.add).then_inc(added, 1)
                    ats = accs[:, bass.ds(start, W)]
                    nc.vector.tensor_tensor(ats, ats, ps[0:2 * MIX, j % MS, MIX * W:(MIX + 1) * W],
                                            ALU.add).then_inc(added, 1)

                for j in range(GPS):
                    masks(j)
                    if j >= MS - 1:
                        add(j - MS + 1)
                for j in range(GPS - MS + 1, GPS):
                    add(j)

        def project(pe, c):
            pe.wait_ge(fa_ready, c + 1)
            if c >= 2:
                pe.wait_ge(res_ready, c - 1)
            for j, a in enumerate(tiles(c)):
                o = ps[:, 4 + c % 2, P * j:P * j + P]
                last = nc.tensor.matmul(o, fa[:, P * j:P * j + P], w2_sb[:, 0, :], start=True, stop=True)
            last.then_inc(out_ready, 1)

        def node_rows(pe, c):
            if c >= 2:
                pe.wait_ge(row_copied, c - 1)
            pe.wait_ge(gu_ready, c + 1)
            for j in range(len(tiles(c))):
                nc.tensor.transpose(ps[:, 4 + c % 2, P * j:P * j + P], ht[:, c % 2, P * j:P * j + P], ident[:, :])
            if c > 0:
                pe.wait_ge(row_copied, c)
            for j in range(len(tiles(c))):
                m = MIX * j
                last = nc.tensor.matmul(ps[:, 6, m:m + MIX], gu[:, P * j:P * j + P],
                                        wb_sb[:, :], start=True, stop=True)
            last.then_inc(rows_ready, 1)
            if c > 0:
                pe.wait_ge(own_added, c)
            pe.wait_ge(gh_ready, c + 1)
            for j in range(len(tiles(c))):
                last = nc.tensor.matmul(ps[:, 7, P * j:P * j + P], gh[:, P * j:P * j + P], w2_sb[:, 1, :],
                                        start=True, stop=True)
            last.then_inc(own_ready, 1)

        def sums(pe, before):
            with pe.Fori(0, STEPS) as i:
                n = before + i
                for j in range(GPS):
                    pe.wait_ge(masks_ready, GPS * n + j + 1)
                    o = ps[:, j % MS, :]
                    for t in range(G):
                        nc.tensor.matmul(o[:, 0:MIX * W], ring[:, G * j + t, 0:D],
                                         mask[:, j % MS, t, 0:MIX, :], start=(t == 0), stop=(t == G - 1))
                    for t in range(G):
                        last = nc.tensor.matmul(o[0:2 * MIX, MIX * W:(MIX + 1) * W], ring[:, G * j + t, D:RS],
                                                mask[:, j % MS, t, MIX, :], start=(t == 0), stop=(t == G - 1))
                    last.then_inc(group_summed, 1)

        def scatter_further(v, before):
            nc.vector.tensor_scalar(base[0:1, :], base[0:1, :], float(W), float(N), ALU.add, ALU.min).then_inc(moved, 1)
            nc.vector.tensor_scalar_add(iota[:, :, :], iota[:, :, :], float(W)).then_inc(moved, 1)
            v.wait_ge(moved, before // STEPS * 2)
            v.nop(nofuse=True)
            scatter(v, before)

        def further_passes(eng, one_pass):
            widest = eng.value_load(span[0:1, 0:1], min_val=0, max_val=N)
            with eng.If(widest >= W):
                with eng.Fori(1, PASSES) as q:
                    with eng.If(widest >= q * W):
                        one_pass(eng, q * STEPS)

        @block.sync
        def _(sp_):
            sp_.dma_start(x_sb[:, XQ[0]:XQ[1], :], x[:, XQ[0]:XQ[1], :]).then_inc(ld_x[0], 16)
            for t, a in ((w1_sb, w1t), (wa_sb, wat), (wb_sb, wbt)):
                sp_.dma_start(t[:, :], a).then_inc(ld_w, 16)
            sp_.dma_start(w2_sb[:, :, :], w2t).then_inc(ld_w, 16)
            sp_.dma_start(b1_sb[:, :], b1).then_inc(ld_w, 16)
            sp_.dma_start(dstg, dst_g).then_inc(ld_dstg, 16)
            for q in range(1, 4):
                sp_.dma_start(x_sb[:, XQ[q]:XQ[q + 1], :], x[:, XQ[q]:XQ[q + 1], :]).then_inc(ld_x[q], 16)
            sp_.dma_start(dst_i[:, :], dst_e).then_inc(ld_dst, 16)
            sp_.dma_start(src_i[:, :], src_e).then_inc(ld_src, 16)
            sp_.dma_start(b2_sb[:, :], b2.to_broadcast([P, D])).then_inc(ld_b2, 16)
            sp_.wait_ge(bounds_ready, 1)
            sp_.dma_start(bounds[0, :].rearrange("(p c) -> p c", c=GC), gmin[:, :]).then_inc(st_bounds, 16)
            sp_.dma_start(bounds[1, :].rearrange("(p c) -> p c", c=GC), gspan[:, :]).then_inc(st_bounds, 16)
            sp_.wait_ge(st_bounds, 32)
            sp_.dma_start(base[:, :], bounds[0:1, :].to_broadcast([P, NG])).then_inc(ld_base, 16)
            sp_.dma_start(spans, bounds[1:2, :]).then_inc(ld_base, 16)
            for c in range(NCH):
                k = len(tiles(c))
                sp_.wait_ge(row_copied, c + 1)
                sp_.dma_start(table[cols(c), :].rearrange("(a p) d -> p a d", p=P),
                              row[:, c % 2, 0:k, :]).then_inc(row_stored[c % 2], 16)
            for c in range(NCH):
                k = len(tiles(c))
                sp_.wait_ge(res_ready, c + 1)
                sp_.dma_start(out[:, 4 * c:4 * c + k, :], res[:, c % 2, 0:k, :]).then_inc(res_stored[c % 2], 16)
            sp_.wait_ge(res_stored[0], 16 * ((NCH + 1) // 2))
            sp_.wait_ge(res_stored[1], 16 * (NCH // 2))

        @block.gpsimd
        def _(pool):
            pool.memset(ident[:, :], 0.0).then_inc(consts, 1)
            pool.memset(sel[:, :, :], 0.0).then_inc(consts, 1)
            pool.memset(down[:, :], 0.0).then_inc(consts, 1)
            pool.iota(iota[:, :, :], [[0, MIX + 1], [1, W]], base=0, channel_multiplier=0,
                      allow_small_or_imprecise_dtypes=True).then_inc(consts, 1)
            pool.wait_ge(consts, 4)
            pool.affine_select(out=ident[:, :], in_=ident[:, :], compare_op=ALU.not_equal, fill=1.0,
                               base=0, pattern=[[-1, P]], channel_multiplier=1).then_inc(consts, 1)
            pool.affine_select(out=sel[:, :, :], in_=sel[:, :, :], compare_op=ALU.not_equal, fill=1.0,
                               base=0, pattern=[[-1, MIX], [0, P]], channel_multiplier=1).then_inc(consts, 1)
            pool.affine_select(out=down[:, :], in_=down[:, :], compare_op=ALU.not_equal, fill=1.0,
                               base=-MIX, pattern=[[-1, MIX]], channel_multiplier=1).then_inc(consts, 1)
            pool.memset(ring[:, :, ROW:RS], 1.0).then_inc(consts, 1)
            pool.memset(accs[:, :], 0.0).then_inc(zeroed, 1)
            pool.memset(acc[:, :, :], 0.0).then_inc(zeroed, 1)
            pool.sem_inc(group_summed, GPS)
            pool.sem_inc(added, 1)
            pool.wait_ge(row_stored[0], 16 * ((NCH + 1) // 2))
            pool.wait_ge(row_stored[1], 16 * (NCH // 2))
            gathers(pool, 0)
            pool.wait_ge(span_ready, 1)
            further_passes(pool, gathers)

        @block.scalar
        def _(act):
            for c in range(NCH):
                k = P * len(tiles(c))
                act.wait_ge(zt_ready, c + 1)
                nc.scalar.activation(hn[:, 0:k], ps[:, c % 2, 0:k], ACT.Relu).then_inc(hn_ready, 1)
                if c == 0:
                    act.wait_ge(ld_w, 80)
                act.wait_ge(h_ready, c + 1)
                if c >= 2:
                    act.wait_ge(own_ready, c - 1)
                nc.scalar.activation(ht[:, c % 2, 0:k], ps[:, 2, 0:k], ACT.Gelu, bias=b1_sb[:, :])\
                    .then_inc(ht_ready, 1)
                act.wait_ge(u_ready, c + 1)
                if c > 0:
                    act.wait_ge(own_ready, c)
                nc.scalar.activation(gu[:, 0:k], ps[:, 3, 0:k], ACT.Gelu).then_inc(gu_ready, 1)
                nc.scalar.activation(gh[:, 0:k], ht[:, c % 2, 0:k], ACT.Gelu).then_inc(gh_ready, 1)
            act.wait_ge(ld_src, 16)
            index_copies(act, 0)
            act.wait_ge(span_ready, 1)
            further_passes(act, index_copies)
            for c in range(NCH):
                k = P * len(tiles(c))
                if c == 0:
                    act.wait_ge(edges_done, 1)
                nc.scalar.activation(acc[:, :, cols(c)], acc[:, :, cols(c)], ACT.Gelu).then_inc(ga_ready, 1)
                if c > 0:
                    node_gelu(act, c - 1)
            node_gelu(act, NCH - 1)

        @block.vector
        def _(v):
            link_count = [0]

            def link(ins):
                ins.then_inc(dve, 1)
                link_count[0] += 1

            def chained():
                v.wait_ge(dve, link_count[0])

            def statistics(a0, a1, part):
                v.wait_ge(ld_x[part], 16)
                for a in range(a0, a1):
                    link(nc.vector.bn_stats(stats[:, a, :], x_sb[:, a, :]))
                chained()
                for a in range(a0, a1):
                    link(nc.vector.bn_aggr(mv[:, a, :], stats[:, a, :]))
                chained()
                var, r = mv[:, a0:a1, 1], rstd[:, a0:a1]
                link(nc.vector.tensor_scalar_add(var, var, EPS))
                chained()
                link(nc.vector.tensor_scalar(r.bitcast(i32), var.bitcast(i32), 1, None, ALU.logical_shift_right))
                chained()
                link(nc.vector.tensor_scalar(r.bitcast(i32), r.bitcast(i32), -1.0, float(RSQRT_BITS),
                                             ALU.mult, ALU.add))
                for _ in range(4):
                    chained()
                    link(nc.vector.tensor_tensor(newton[:, a0:a1], r, r, ALU.mult))
                    chained()
                    link(nc.vector.scalar_tensor_tensor(newton[:, a0:a1], newton[:, a0:a1], -0.5, var,
                                                        ALU.mult, ALU.mult))
                    chained()
                    link(nc.vector.scalar_tensor_tensor(r, newton[:, a0:a1], 1.5, r, ALU.add, ALU.mult))
                chained()

            v.wait_ge(ld_dstg, 16)
            nc.vector.tensor_reduce(gmin[:, :], dstg, axis=AX.X, op=ALU.min)
            link(nc.vector.tensor_reduce(gmax[:, :], dstg, axis=AX.X, op=ALU.max))
            chained()
            nc.vector.tensor_tensor(gspan[:, :], gmax[:, :], gmin[:, :], ALU.subtract).then_inc(bounds_ready, 1)
            for c in range(NCH):
                k = len(tiles(c))
                if 4 * c in XQ:
                    statistics(XQ[x_part(c)], XQ[x_part(c) + 1], x_part(c))
                if c > 0:
                    v.wait_ge(zt_ready, c)
                for j, a in enumerate(tiles(c)):
                    last = nc.vector.tensor_scalar(z[:, j, :], x_sb[:, a, :], mv[:, a, 0:1], rstd[:, a:a + 1],
                                                   ALU.subtract, ALU.mult)
                last.then_inc(z_ready, 1)
                if c == 0:
                    v.wait_ge(ld_b2, 16)
                v.wait_ge(z_ready, c + 1)
                link(nc.vector.tensor_tensor(x_sb[:, 4 * c:4 * c + k, :], x_sb[:, 4 * c:4 * c + k, :],
                                             b2_sb[:, None, :].to_broadcast([P, k, D]), ALU.add))
                if c > 0:
                    table_rows(v, c - 1)
            chained()
            table_rows(v, NCH - 1)
            v.wait_ge(ld_base, 32)
            nc.vector.tensor_reduce(span[:, :], spans, axis=AX.X, op=ALU.max).then_inc(span_ready, 1)
            v.wait_ge(ld_dst, 16)
            link(nc.vector.tensor_tensor(dloc.rearrange("p (g t) -> p g t", t=G),
                                         dst_i[:, :].rearrange("p (g t) -> p g t", t=G),
                                         base[:, :, None].to_broadcast([P, NG, G]), ALU.subtract))
            v.wait_ge(consts, 8)
            v.wait_ge(zeroed, 2)
            chained()
            scatter(v, 0)
            v.wait_ge(span_ready, 1)
            further_passes(v, scatter_further)
            nc.vector.memset(newton[:, 0:1], 0.0).then_inc(edges_done, 1)
            for c in range(NCH):
                k = P * len(tiles(c))
                v.wait_ge(counts_ready, c + 1)
                link(nc.vector.tensor_scalar_max(sp[:, 0:k], ps[0:MIX, 6, 0:k], 1.0))
                chained()
                link(nc.vector.reciprocal(sp[:, 0:k], sp[:, 0:k]))
                chained()
                nc.vector.tensor_tensor(sp[:, 0:k], sp[:, 0:k], accs[0:MIX, cols(c)], ALU.mult).then_inc(sp_ready, 1)
                v.wait_ge(ga_ready, c + 1)
                v.wait_ge(spread, c + 1)
                if c > 0:
                    v.wait_ge(fa_ready, c)
                link(nc.vector.tensor_tensor(prod[:, :, 0:k], acc[:, :, cols(c)], ps[:, 0:MIX, 0:k], ALU.mult))
                chained()
                link(nc.vector.tensor_tensor(prod[:, 0:2, 0:k], prod[:, 0:2, 0:k], prod[:, 2:4, 0:k], ALU.add))
                chained()
                nc.vector.tensor_tensor(prod[:, 0, 0:k], prod[:, 0, 0:k], prod[:, 1, 0:k],
                                        ALU.add).then_inc(node_ready, 1)
                if c > 0:
                    results(v, c - 1)
            results(v, NCH - 1)

        @block.tensor
        def _(pe):
            pe.wait_ge(consts, 8)
            for c in range(NCH):
                k = len(tiles(c))
                pe.wait_ge(z_ready, c + 1)
                if c >= 2:
                    pe.wait_ge(hn_ready, c - 1)
                for j in range(k):
                    last = nc.tensor.transpose(ps[:, c % 2, P * j:P * j + P], z[:, j, :], ident[:, :])
                last.then_inc(zt_ready, 1)
                if c > 0:
                    node_rows(pe, c - 1)
                if c == 0:
                    pe.wait_ge(ld_w, 80)
                pe.wait_ge(hn_ready, c + 1)
                nc.tensor.matmul(ps[:, 2, 0:P * k], w1_sb[:, :], hn[:, 0:P * k], start=True, stop=True)\
                    .then_inc(h_ready, 1)
                pe.wait_ge(ht_ready, c + 1)
                nc.tensor.matmul(ps[:, 3, 0:P * k], wa_sb[:, :], ht[:, c % 2, 0:P * k], start=True, stop=True)\
                    .then_inc(u_ready, 1)
            node_rows(pe, NCH - 1)
            sums(pe, 0)
            pe.wait_ge(span_ready, 1)
            further_passes(pe, sums)
            for c in range(NCH):
                k = len(tiles(c))
                if c == 0:
                    pe.wait_ge(edges_done, 1)
                else:
                    pe.wait_ge(sp_ready, c)
                nc.tensor.matmul(ps[0:MIX, 6, 0:P * k], down[:, :], accs[:, cols(c)], start=True, stop=True)\
                    .then_inc(counts_ready, 1)
                pe.wait_ge(sp_ready, c + 1)
                if c > 0:
                    pe.wait_ge(node_ready, c)
                for m in range(MIX):
                    last = nc.tensor.matmul(ps[:, m, 0:P * k], sel[:, m, :], sp[:, 0:P * k], start=True, stop=True)
                last.then_inc(spread, 1)
                if c > 0:
                    project(pe, c - 1)
            project(pe, NCH - 1)

_OUT = "out_dram"


def kernel(x, src, dst, L0_gnn_W1, L0_gnn_b1, L0_gnn_WA, L0_gnn_WB, L0_gnn_W2, L0_gnn_b2):
    import numpy as _np
    import concourse.bacc as _bacc
    from concourse import mybir as _mybir
    from concourse.bass_utils import run_bass_kernel_spmd as _run

    def by_partition(a):
        return _np.ascontiguousarray(a.reshape(-1, P, *a.shape[1:]).swapaxes(0, 1))

    x, src, dst = _np.asarray(x), _np.asarray(src), _np.asarray(dst)
    w2 = _np.asarray(L0_gnn_W2)
    pad = ET * P - E
    laid_out = {
        "x": by_partition(_np.pad(x, ((0, NT * P - N), (0, 0)))),
        "src_by_edge": by_partition(_np.pad(src, (0, pad))),
        "dst_by_edge": by_partition(_np.pad(dst, (0, pad), constant_values=PAD_DST)),
        "dst_by_group": _np.pad(dst, (0, pad), mode="edge").reshape(GP, GC, G * P),
        "W1t": _np.asarray(L0_gnn_W1).T,
        "b1": _np.asarray(L0_gnn_b1).reshape(D, 1),
        "WAt": _np.asarray(L0_gnn_WA).T,
        "WBt": _np.asarray(L0_gnn_WB).T,
        "W2t": w2.T.reshape(2, D, D).swapaxes(0, 1),
        "b2": _np.asarray(L0_gnn_b2).reshape(1, D),
    }
    nc = _bacc.Bacc("TRN2", target_bir_lowering=False, num_devices=1)
    arrays, args = {}, []
    for name, a in laid_out.items():
        arrays[f"in_{name}"] = a = _np.ascontiguousarray(a)
        args.append(nc.dram_tensor(f"in_{name}", a.shape, _mybir.dt.from_np(a.dtype), kind="ExternalInput").ap())
    out = nc.dram_tensor(_OUT, (P, NT, D), _mybir.dt.float32, kind="ExternalOutput").ap()
    gnn_kernel(nc, *args, out)
    r = _run(nc, [arrays], core_ids=[0])
    return r.results[0][_OUT].swapaxes(0, 1).reshape(NT * P, D)[:N]
```

```python
import concourse.bass as bass
from concourse import mybir
from contextlib import ExitStack
from functools import partial

P = 128
N = 6250
E = 200000
D = 128
MIX = 4
NT = -(-N // P)
NCH = -(-NT // 4)
G = 2
GPS = 7
U = GPS * G
STEPS = -(-E // (P * U))
ET = STEPS * U
NG = ET // G
GP = 112
GC = NG // GP
W = 24
PASSES = -(-N // W)
NACC = N + W
MS = 3
ROW = D + MIX
RS = ROW + 1
PAD_DST = 1 << 20
CG = 4
CT = NT * CG * G
CN = 416
CW = 8
AW = CN + CW
PL = MIX + 1
SPL = 3
EXACT = 256
AB = 7
NAB = NT // AB
S1 = NT
S2 = PL * NAB
assert CT + (S1 + S2) * U == ET and NAB * AB == NT and AB <= GPS
EPS = 1e-5
RSQRT_BITS = 0x5F3759DF
assert NG == GP * GC and NACC >= NT * P


def gnn_kernel(nc, x, src_e, dst_e, dst_g, w1t, b1, wat, wbt, w2t, b2, out):
    f32 = mybir.dt.float32
    i32 = mybir.dt.int32
    i16 = mybir.dt.int16
    bf16 = mybir.dt.bfloat16
    f16 = mybir.dt.float16
    ALU = mybir.AluOpType
    ACT = mybir.ActivationFunctionType
    AX = mybir.AxisListType

    ctx = ExitStack()
    with ctx:
        def sb(name, shape, dt=f32):
            return ctx.enter_context(nc.sbuf_tensor(name, shape, dt))

        def sem(name):
            return ctx.enter_context(nc.semaphore(name))

        table = nc.dram_tensor("node_table", [NT * P, ROW], f32, kind="Internal").ap()
        parts = nc.dram_tensor("product_parts", [PL, NT, P, SPL * P], bf16, kind="Internal").ap()
        own = nc.dram_tensor("own_part", [P, NT, D], f32, kind="Internal").ap()
        most_d = nc.dram_tensor("largest_counts", [P], f32, kind="Internal").ap()
        sums_d = nc.dram_tensor("mix_sums", [MIX + 1, NT * P], f32, kind="Internal").ap()
        weights_d = nc.dram_tensor("mix_weights", [MIX, NT * P], f32, kind="Internal").ap()
        bounds = nc.dram_tensor("window_bounds", [2, NG], i32, kind="Internal").ap()

        counts = sb("counts", [P, NT, AW], bf16)
        x_sb = counts[:, :, :].rearrange("p a n -> p (a n)").bitcast(f32)[:, 0:NT * D]\
            .rearrange("p (a d) -> p a d", d=D)
        words = counts[:, :, :].rearrange("p a n -> p (a n)").bitcast(f32)

        def behind_x(at, size):
            return words[:, NT * D + at:NT * D + at + size]

        ident = behind_x(0, P)
        w1_sb = behind_x(P, D)
        wa_sb = behind_x(P + D, D)
        w2b_sb = behind_x(P + 2 * D, D)
        b2_sb = behind_x(P + 3 * D, D)
        rstd = behind_x(P + 4 * D, NT)
        mv = behind_x(P + 4 * D + NT, 2 * NT).rearrange("p (a s) -> p a s", s=2)
        res = behind_x(0, 8 * D).rearrange("p (b a d) -> p b a d", b=2, a=4)
        sums_n = behind_x(8 * D, PL * NT).rearrange("p (m a) -> p m a", m=PL)
        weights_n = behind_x(8 * D + PL * NT, MIX * NT).rearrange("p (m a) -> p m a", m=MIX)
        xr = [x_sb[:, 4 * i:4 * i + 4, :] for i in (0, 1, 2)]
        acc = sb("acc", [P, PL, NACC])
        accs = acc[0:PL, MIX, :]
        edges = sb("edges", [P, 2, ET], i32)
        src_i, dst_i = edges[:, 0, :], edges[:, 1, :]
        dloc = dst_i.bitcast(f32)
        gmin = sb("gmin", [GP, GC], i32)
        gmax = sb("gmax", [GP, GC], i32)
        gspan = sb("gspan", [GP, GC], i32)
        key_a = sb("key_a", [P, CT])
        key_b = sb("key_b", [P, CT])
        zero = sb("zero", [P, P], bf16)
        iota_a = sb("iota_a", [P, NT * CW], f16)
        iota_b = sb("iota_b", [P, P], bf16)
        hot_a = sb("hot_a", [P, 2, G, NT * CW], bf16)
        hot_b = sb("hot_b", [P, 2, G, P], bf16)
        most = sb("most", [P, NAB])
        most_p = sb("most_p", [P, 1])
        marks = sb("marks", [1, 4])
        flag = sb("flag", [1, 1], i32)
        span = sb("span", [1, 1], i32)
        idx = sb("idx", [P, U], i32)
        ring = sb("ring", [P, U, RS])
        mask = sb("mask", [P, MS, G, MIX + 1, W])
        iota = sb("iota", [P, MIX + 1, W])
        wb_sb = sb("wb_sb", [P, MIX])
        w2a_sb = sb("w2a_sb", [P, D])
        b1_sb = sb("b1_sb", [P, 1])
        done = sb("done", [P, 1])
        row = sb("row", [P, 2, 4, ROW])
        work = acc[:, MIX - 1, 0:12 * 4 * P].rearrange("p (k n) -> p k n", k=12)
        z = [work[:, i, :].rearrange("p (a d) -> p a d", d=D) for i in (0, 1)]
        hn = [work[:, i, :] for i in (2, 3)]
        ht = [work[:, i, :] for i in (4, 5, 6)]
        gu = [work[:, i, :] for i in (7, 8)]
        gh = [work[:, i, :] for i in (9, 10)]
        stats = work[:, 11, 0:6 * NT].rearrange("p (a s) -> p a s", s=6)
        newton = work[:, 11, 6 * NT:7 * NT]
        room = sb("room", [P, MIX * 4 * P])
        dstg = room[0:GP, 0:GC * G * P].bitcast(i32).rearrange("p (c e) -> p c e", c=GC)
        base_b = room[:, 0:NG].bitcast(i32)
        spans = room[0:1, NG:2 * NG].bitcast(i32)
        tops = room[0:1, 2 * NG:2 * NG + S1 * CG]
        cf = room[:, 0:PL * P].rearrange("p (m d) -> p m d", m=PL)
        rest = room[:, PL * P:2 * PL * P].rearrange("p (m d) -> p m d", m=PL)
        crow = room[:, 2 * PL * P:2 * PL * P + ROW]
        most_r = room[0:1, 2 * PL * P + ROW:2 * PL * P + ROW + P]
        c3 = row[:, :, :, :].rearrange("p b a d -> p (b a d)").bitcast(bf16)[:, 0:PL * SPL * P]\
            .rearrange("p (m s d) -> p m s d", m=PL, s=SPL)
        after_most = 2 * PL * P + ROW + P
        base = room[0:1, after_most:after_most + NG // 2].bitcast(i16)
        base_c = room[0:1, after_most + NG // 2:after_most + (NG + S1 * CG) // 2].bitcast(i16)
        cbuf = room[:, :].bitcast(bf16)[:, 0:AB * SPL * P].rearrange("p (a s d) -> p a s d", a=AB, s=SPL)
        fa = [row[:, i, :, :].rearrange("p a d -> p (a d)") for i in (0, 1)]
        spread = [t[:, 0:MIX * 4 * P].rearrange("p (m n) -> p m n", m=MIX) for t in
                  (room[:, :], words[:, 12 * D:28 * D], words[:, 28 * D:44 * D])]

        ps = ctx.enter_context(nc.psum_tensor("ps", [P, 8, 512], f32))

        XQ = [0, 4, 12, 20, 28, 36, 44, NT]
        XP = len(XQ) - 1
        ld_x = [sem(f"ld_x{i}") for i in range(XP)]
        ld_w = sem("ld_w")
        ld_b2 = sem("ld_b2")
        ld_src = sem("ld_src")
        ld_dst = sem("ld_dst")
        ld_dstg = sem("ld_dstg")
        consts = sem("consts")
        zeroed = sem("zeroed")
        dve = sem("dve_chain")
        st_bounds = sem("st_bounds")
        ld_base = sem("ld_base")
        b2_added = sem("b2_added")
        bounds_ready = sem("bounds_ready")
        z_ready = sem("z_ready")
        zt_ready = sem("zt_ready")
        hn_ready = sem("hn_ready")
        h_ready = sem("h_ready")
        ht_ready = sem("ht_ready")
        u_ready = sem("u_ready")
        gu_ready = sem("gu_ready")
        rows_ready = sem("rows_ready")
        t_copied = sem("t_copied")
        h_copied = sem("h_copied")
        row_stored = [sem(f"row_stored{i}") for i in range(2)]
        idx_ready = sem("idx_ready")
        gathered = [sem(f"gathered{i}") for i in range(U)]
        masks_ready = sem("masks_ready")
        group_summed = sem("group_summed")
        added = sem("added")
        own_stored = [sem(f"own_stored{i}") for i in range(2)]
        own_loaded = [sem(f"own_loaded{i}") for i in range(3)]
        marks_ready = sem("marks_ready")
        plane_set = sem("plane_set")
        hots_ready = sem("hots_ready")
        counted = sem("counted")
        counts_added = sem("counts_added")
        crow_loaded = sem("crow_loaded")
        products_made = sem("products_made")
        part_hi = sem("part_hi")
        rest_made = sem("rest_made")
        part_mid = sem("part_mid")
        part_lo = sem("part_lo")
        parts_stored = sem("parts_stored")
        parts_free = sem("parts_free")
        cbuf_loaded = sem("cbuf_loaded")
        multiplied = sem("multiplied")
        product_added = sem("product_added")
        most_made = sem("most_made")
        most_ready = sem("most_ready")
        most_stored = sem("most_stored")
        most_loaded = sem("most_loaded")
        moved = sem("moved")
        cleared = sem("cleared")
        flag_ready = sem("flag_ready")
        edges_done = sem("edges_done")
        own_ready = sem("own_ready")
        own_added = sem("own_added")
        gh_ready = sem("gh_ready")
        ga_ready = sem("ga_ready")
        sums_stored = sem("sums_stored")
        sums_loaded = sem("sums_loaded")
        weights_ready = sem("weights_ready")
        weights_stored = sem("weights_stored")
        spread_loaded = [sem(f"spread_loaded{i}") for i in range(3)]
        prod_ready = sem("prod_ready")
        pair_ready = sem("pair_ready")
        node_ready = sem("node_ready")
        fa_ready = sem("fa_ready")
        out_ready = sem("out_ready")
        res_ready = sem("res_ready")
        res_stored = [sem(f"res_stored{i}") for i in range(2)]

        block = ctx.enter_context(nc.Block())

        def tiles(c):
            return range(4 * c, min(4 * c + 4, NT))

        def cols(c):
            return slice(512 * c, 512 * c + P * len(tiles(c)))


        def x_part(c):
            return next(q for q in range(XP) if 4 * c < XQ[q + 1])


        def gather_step(pool, n):
            for j in range(GPS):
                pool.wait_ge(idx_ready, GPS * n + j + 1)
                pool.nop(nofuse=True)
                for s in range(G * j, G * j + G):
                    pool.indirect_dma_start(
                        out=ring[:, s, 0:ROW], out_offset=None, in_=table,
                        in_offset=bass.IndirectOffsetOnAxis(ap=idx[:, s:s + 1], axis=0),
                    ).then_inc(gathered[s], 16)

        def index_copy(act, tile, n, j):
            act.wait_ge(group_summed, GPS * n + j + 1)
            nc.scalar.activation(idx[:, G * j:G * j + G], src_i[:, bass.ds(tile + G * j, G)],
                                 ACT.Copy).then_inc(idx_ready, 1)

        def h_rows(act, c):
            k = len(tiles(c))
            act.wait_ge(rows_ready, c + 1)
            if c >= 2:
                act.wait_ge(row_stored[c % 2], 16 * (c // 2))
            nc.scalar.activation(row[:, c % 2, 0:k, 0:D],
                                 ps[:, 4 + c % 2, 0:P * k].rearrange("p (a d) -> p a d", d=D),
                                 ACT.Copy).then_inc(h_copied, 1)

        def node_gelu(act, c):
            k = P * len(tiles(c))
            act.wait_ge(node_ready, c + 1)
            if c >= 2:
                act.wait_ge(out_ready, c - 1)
            nc.scalar.activation(fa[c % 2][:, 0:k], acc[:, 0, cols(c)], ACT.Gelu).then_inc(fa_ready, 1)

        def results(v, c):
            k = len(tiles(c))
            v.wait_ge(out_ready, c + 1)
            v.wait_ge(own_loaded[c % 3], 16 * (c // 3 + 1))
            if c >= 2:
                v.wait_ge(res_stored[c % 2], 16 * (c // 2))
            nc.vector.tensor_tensor(res[:, c % 2, 0:k, :],
                                    ps[:, 4 + c % 2, 0:P * k].rearrange("p (a d) -> p a d", d=D),
                                    xr[c % 3][:, 0:k, :], ALU.add).then_inc(res_ready, 1)

        def table_rows(v, c):
            k = len(tiles(c))
            v.wait_ge(rows_ready, c + 1)
            if c >= 2:
                v.wait_ge(row_stored[c % 2], 16 * (c // 2))
            nc.vector.tensor_copy(row[:, c % 2, 0:k, D:ROW],
                                  ps[:, 6, 0:MIX * k].rearrange("p (a m) -> p a m", m=MIX))\
                .then_inc(t_copied, 1)
            v.wait_ge(own_ready, c + 1)
            v.wait_ge(b2_added, c + 1)
            nc.vector.tensor_tensor(x_sb[:, 4 * c:4 * c + k, :], x_sb[:, 4 * c:4 * c + k, :],
                                    ps[:, 7, 0:P * k].rearrange("p (a d) -> p a d", d=D),
                                    ALU.add).then_inc(own_added, 1)

        def window_starts(v, regs, row, first, largest):
            v.load(regs, row[:, bass.ds(first, len(regs))])
            return [v.snap(reg, min_val=0, max_val=largest) for reg in regs]

        start_regs = [nc.vector.alloc_register(f"start_{j}") for j in range(GPS)]
        start_regs_c = [nc.vector.alloc_register(f"start_in_a_{g}") for g in range(CG)]

        def scatter_step(v, tile, group, n, between):
            def masks(j):
                for t in range(G):
                    s = G * j + t
                    v.wait_ge(gathered[s], 16 * n + 16)
                    last = nc.vector.scalar_tensor_tensor(
                        mask[:, j % MS, t, :, :], iota[:, :, :], dloc[:, bass.ds(tile + s, 1)],
                        ring[:, s, D:D + MIX + 1][:, :, None].to_broadcast([P, MIX + 1, W]),
                        ALU.is_equal, ALU.mult)
                last.then_inc(masks_ready, 1)

            starts = window_starts(v, start_regs, base, group, N)

            def add(j):
                v.wait_ge(group_summed, GPS * n + GPS + j + 1)
                v.wait_ge(added, GPS * n + j + 1)
                at = acc[:, :, bass.ds(starts[j], W)]
                nc.vector.tensor_tensor(at, at, ps[:, j % MS, 0:PL * W].rearrange("p (m w) -> p m w", w=W),
                                        ALU.add).then_inc(added, 1)

            for j in range(GPS):
                masks(j)
                if j >= MS - 1:
                    add(j - MS + 1)
                if j in between:
                    between[j]()
            for j in range(GPS - MS + 1, GPS):
                add(j)

        def hots(v, i, g):
            for t in range(G):
                at = bass.ds(G * (CG * i + g) + t, 1)
                nc.vector.tensor_scalar(hot_b[:, g % 2, t, :], iota_b[:, :], key_b[:, at], None, ALU.is_equal)
                last = nc.vector.tensor_scalar(hot_a[:, g % 2, t, :], iota_a[:, :], key_a[:, at], None, ALU.is_equal)
            last.then_inc(hots_ready, 1)

        def add_counts(v, i, g, starts):
            v.wait_ge(counted, CG * i + g + 1)
            v.wait_ge(counts_added, CG * i + g + 1)
            at = counts[:, :, bass.ds(starts[g], CW)]
            nc.vector.tensor_tensor(at, at, ps[:, 3 + g % 2, 0:NT * CW].rearrange("p (a w) -> p a w", w=CW),
                                    ALU.add).then_inc(counts_added, 1)

        def project(pe, c):
            pe.wait_ge(fa_ready, c + 1)
            if c >= 2:
                pe.wait_ge(res_ready, c - 1)
            for j, a in enumerate(tiles(c)):
                o = ps[:, 4 + c % 2, P * j:P * j + P]
                last = nc.tensor.matmul(o, fa[c % 2][:, P * j:P * j + P], w2a_sb[:, :], start=True, stop=True)
            last.then_inc(out_ready, 1)

        def node_rows(pe, c):
            if c >= 2:
                pe.wait_ge(h_copied, c - 1)
            pe.wait_ge(gu_ready, c + 1)
            for j in range(len(tiles(c))):
                nc.tensor.transpose(ps[:, 4 + c % 2, P * j:P * j + P], ht[c % 3][:, P * j:P * j + P], ident)
            if c > 0:
                pe.wait_ge(t_copied, c)
            for j in range(len(tiles(c))):
                m = MIX * j
                last = nc.tensor.matmul(ps[:, 6, m:m + MIX], gu[c % 2][:, P * j:P * j + P],
                                        wb_sb[:, :], start=True, stop=True)
            last.then_inc(rows_ready, 1)
            if c > 0:
                pe.wait_ge(own_added, c)
            pe.wait_ge(gh_ready, c + 1)
            for j in range(len(tiles(c))):
                last = nc.tensor.matmul(ps[:, 7, P * j:P * j + P], gh[c % 2][:, P * j:P * j + P], w2b_sb,
                                        start=True, stop=True)
            last.then_inc(own_ready, 1)

        def sum_step(pe, n, between):
            for j in range(GPS):
                pe.wait_ge(masks_ready, GPS * n + j + 1)
                o = ps[:, j % MS, :]
                for t in range(G):
                    nc.tensor.matmul(o[:, 0:MIX * W], ring[:, G * j + t, 0:D],
                                     mask[:, j % MS, t, 0:MIX, :], start=(t == 0), stop=(t == G - 1))
                for t in range(G):
                    last = nc.tensor.matmul(o[0:PL, MIX * W:(MIX + 1) * W], ring[:, G * j + t, D:RS],
                                            mask[:, j % MS, t, MIX, :], start=(t == 0), stop=(t == G - 1))
                last.then_inc(group_summed, 1)
                if j in between:
                    between[j]()

        def count(pe, i, g):
            pe.wait_ge(hots_ready, CG * i + g + 1)
            for t in range(G):
                last = nc.tensor.matmul(ps[:, 3 + g % 2, 0:NT * CW], hot_b[:, g % 2, t, :], hot_a[:, g % 2, t, :],
                                        start=(t == 0), stop=(t == G - 1))
            last.then_inc(counted, 1)

        def general_path(eng, step):
            eng.wait_ge(flag_ready, 1)
            flagged = eng.value_load(flag[0:1, 0:1], min_val=0, max_val=1)
            with eng.If(flagged >= 1):
                widest = eng.value_load(span[0:1, 0:1], min_val=0, max_val=N)
                with eng.Fori(0, PASSES) as q:
                    with eng.If(widest >= q * W):
                        with eng.Fori(0, STEPS) as i:
                            step(eng, i, S1 + S2 + q * STEPS + i)

        def table_stored(eng):
            eng.wait_ge(row_stored[0], 16 * ((NCH + 1) // 2))
            eng.wait_ge(row_stored[1], 16 * (NCH // 2))

        def load_parts(sp_, m0, m1):
            with sp_.Fori(m0, m1) as m:
                with sp_.Fori(0, NAB) as ab:
                    sp_.wait_ge(multiplied, NAB * m + ab + 1)
                    sp_.dma_start(cbuf.rearrange("p a s d -> p a (s d)"),
                                  parts[bass.ds(m, 1), bass.ds(AB * ab, AB), :, :]
                                  .rearrange("m a p x -> p (m a) x")).then_inc(cbuf_loaded, 16)

        def store(sp_, c):
            k = len(tiles(c))
            sp_.wait_ge(res_ready, c + 1)
            sp_.dma_start(out[:, 4 * c:4 * c + k, :], res[:, c % 2, 0:k, :]).then_inc(res_stored[c % 2], 16)

        @block.sync
        def _(sp_):
            sp_.dma_start(x_sb[:, XQ[0]:XQ[1], :], x[:, XQ[0]:XQ[1], :]).then_inc(ld_x[0], 16)
            sp_.dma_start(x_sb[:, XQ[1]:XQ[2], :], x[:, XQ[1]:XQ[2], :]).then_inc(ld_x[1], 16)
            for t, a in ((w1_sb, w1t), (wa_sb, wat), (wb_sb[:, :], wbt)):
                sp_.dma_start(t, a).then_inc(ld_w, 16)
            sp_.dma_start(w2a_sb[:, :], w2t[:, 0, :]).then_inc(ld_w, 16)
            sp_.dma_start(w2b_sb, w2t[:, 1, :]).then_inc(ld_w, 16)
            sp_.dma_start(b1_sb[:, :], b1).then_inc(ld_w, 16)
            sp_.dma_start(dstg, dst_g).then_inc(ld_dstg, 16)
            for q in range(2, XP):
                sp_.dma_start(x_sb[:, XQ[q]:XQ[q + 1], :], x[:, XQ[q]:XQ[q + 1], :]).then_inc(ld_x[q], 16)
            sp_.dma_start(dst_i, dst_e).then_inc(ld_dst, 16)
            sp_.dma_start(src_i, src_e).then_inc(ld_src, 16)
            sp_.dma_start(b2_sb, b2.to_broadcast([P, D])).then_inc(ld_b2, 16)
            sp_.wait_ge(bounds_ready, 1)
            sp_.dma_start(bounds[0, :].rearrange("(p c) -> p c", c=GC), gmin[:, :]).then_inc(st_bounds, 16)
            sp_.dma_start(bounds[1, :].rearrange("(p c) -> p c", c=GC), gspan[:, :]).then_inc(st_bounds, 16)
            sp_.wait_ge(st_bounds, 32)
            sp_.dma_start(base_b, bounds[0:1, :].to_broadcast([P, NG])).then_inc(ld_base, 16)
            sp_.dma_start(spans, bounds[1:2, :]).then_inc(ld_base, 16)
            for c in range(NCH):
                k = len(tiles(c))
                sp_.wait_ge(h_copied, c + 1)
                sp_.wait_ge(t_copied, c + 1)
                sp_.dma_start(table[cols(c), :].rearrange("(a p) d -> p a d", p=P),
                              row[:, c % 2, 0:k, :]).then_inc(row_stored[c % 2], 16)
                sp_.wait_ge(own_added, c + 1)
                sp_.dma_start(own[:, 4 * c:4 * c + k, :], x_sb[:, 4 * c:4 * c + k, :])\
                    .then_inc(own_stored[c % 2], 16)
            sp_.sem_inc(parts_free, 1)
            table_stored(sp_)
            sp_.wait_ge(marks_ready, 1)
            sp_.dma_start(crow, table[0:P, :]).then_inc(crow_loaded, 16)
            with sp_.Fori(1, NT) as i:
                sp_.wait_ge(products_made, i)
                sp_.dma_start(crow, table[bass.ds(P * i, P), :]).then_inc(crow_loaded, 16)
                sp_.wait_ge(part_lo, i)
                sp_.dma_start(parts[:, bass.ds(i - 1, 1), :, :].rearrange("m a p x -> p (m a) x"),
                              c3.rearrange("p m s d -> p m (s d)")).then_inc(parts_stored, 16)
                sp_.wait_ge(parts_stored, 16 * i)
                sp_.sem_inc(parts_free, 1)
            sp_.wait_ge(part_lo, NT)
            sp_.dma_start(parts[:, NT - 1, :, :].rearrange("m p x -> p m x"),
                          c3.rearrange("p m s d -> p m (s d)")).then_inc(parts_stored, 16)
            sp_.wait_ge(parts_stored, 16 * NT)
            load_parts(sp_, 0, 1)
            sp_.wait_ge(most_ready, 1)
            sp_.dma_start(most_d.rearrange("(p a) -> p a", a=1), most_p[:, :]).then_inc(most_stored, 16)
            sp_.wait_ge(most_stored, 16)
            sp_.dma_start(most_r, most_d.rearrange("(a p) -> a p", a=1)).then_inc(most_loaded, 16)
            load_parts(sp_, 1, PL)
            sp_.wait_ge(edges_done, 1)
            sp_.dma_start(sums_d, accs[:, 0:NT * P]).then_inc(sums_stored, 16)
            sp_.wait_ge(sums_stored, 16)
            sp_.dma_start(sums_n, sums_d.rearrange("r (p a) -> p r a", a=NT)).then_inc(sums_loaded, 16)
            sp_.wait_ge(weights_ready, 1)
            sp_.dma_start(weights_d.rearrange("m (p a) -> p m a", a=NT), weights_n)\
                .then_inc(weights_stored, 16)
            sp_.wait_ge(weights_stored, 16)
            for c in range(NCH + 4):
                if c < NCH:
                    if c >= 3:
                        sp_.wait_ge(prod_ready, c - 2)
                    sp_.dma_start(spread[c % 3][:, :, 0:P * len(tiles(c))],
                                  weights_d[None, :, cols(c)].to_broadcast([P, MIX, P * len(tiles(c))]))\
                        .then_inc(spread_loaded[c % 3], 16)
                    if c >= 3:
                        sp_.wait_ge(res_ready, c - 2)
                    sp_.dma_start(xr[c % 3][:, 0:len(tiles(c)), :], own[:, 4 * c:4 * c + len(tiles(c)), :])\
                        .then_inc(own_loaded[c % 3], 16)
                if c >= 4:
                    store(sp_, c - 4)
            sp_.wait_ge(res_stored[0], 16 * ((NCH + 1) // 2))
            sp_.wait_ge(res_stored[1], 16 * (NCH // 2))

        @block.gpsimd
        def _(pool):
            pool.memset(ident, 0.0).then_inc(consts, 1)
            pool.iota(iota[:, :, :], [[0, MIX + 1], [1, W]], base=0, channel_multiplier=0,
                      allow_small_or_imprecise_dtypes=True).then_inc(consts, 1)
            pool.iota(iota_a[:, :], [[1, NT * CW]], base=0, channel_multiplier=0,
                      allow_small_or_imprecise_dtypes=True).then_inc(consts, 1)
            pool.iota(iota_b[:, :], [[1, P]], base=0, channel_multiplier=0,
                      allow_small_or_imprecise_dtypes=True).then_inc(consts, 1)
            pool.wait_ge(consts, 4)
            pool.affine_select(out=ident, in_=ident, compare_op=ALU.not_equal, fill=1.0,
                               base=0, pattern=[[-1, P]], channel_multiplier=1).then_inc(consts, 1)
            pool.memset(ring[:, :, ROW:RS], 1.0).then_inc(consts, 1)
            pool.memset(zero[:, :], 0.0).then_inc(consts, 1)
            pool.memset(acc[:, MIX, :], 0.0).then_inc(zeroed, 1)
            pool.memset(acc[:, 0:MIX - 1, :], 0.0).then_inc(zeroed, 1)
            pool.wait_ge(ld_b2, 16)
            for c in range(NCH):
                k = len(tiles(c))
                pool.wait_ge(z_ready, c + 1)
                pool.tensor_tensor(x_sb[:, 4 * c:4 * c + k, :], x_sb[:, 4 * c:4 * c + k, :],
                                   b2_sb[:, None, :].to_broadcast([P, k, D]), ALU.add).then_inc(b2_added, 1)
            pool.sem_inc(group_summed, GPS)
            for first in (added, counts_added, rest_made, multiplied, product_added):
                pool.sem_inc(first, 1)
            table_stored(pool)
            with pool.Fori(0, S1 + S2) as i:
                gather_step(pool, i)
            general_path(pool, lambda eng, i, n: gather_step(eng, n))
            for c in range(NCH):
                pool.wait_ge(prod_ready, c + 1)
                pool.tensor_tensor(acc[:, 0:2, cols(c)], acc[:, 0:2, cols(c)], acc[:, 2:4, cols(c)],
                                   ALU.add).then_inc(pair_ready, 1)

        @block.scalar
        def _(act):
            act.wait_ge(ld_w, 96)
            for c in range(NCH + 3):
                if c < NCH:
                    k = P * len(tiles(c))
                    act.wait_ge(zt_ready, c + 1)
                    if c >= 2:
                        act.wait_ge(h_ready, c - 1)
                    nc.scalar.activation(hn[c % 2][:, 0:k], ps[:, c % 2, 0:k], ACT.Relu).then_inc(hn_ready, 1)
                if 1 <= c < NCH + 1:
                    b = c - 1
                    k = P * len(tiles(b))
                    act.wait_ge(h_ready, b + 1)
                    if b >= 3:
                        act.wait_ge(rows_ready, b - 2)
                    nc.scalar.activation(ht[b % 3][:, 0:k], ps[:, 2, 0:k], ACT.Gelu, bias=b1_sb[:, :])\
                        .then_inc(ht_ready, 1)
                if c >= 3:
                    h_rows(act, c - 3)
                if 2 <= c < NCH + 2:
                    b = c - 2
                    k = P * len(tiles(b))
                    act.wait_ge(u_ready, b + 1)
                    if b >= 2:
                        act.wait_ge(own_ready, b - 1)
                    nc.scalar.activation(gu[b % 2][:, 0:k], ps[:, 3, 0:k], ACT.Gelu).then_inc(gu_ready, 1)
                    nc.scalar.activation(gh[b % 2][:, 0:k], ht[b % 3][:, 0:k], ACT.Gelu).then_inc(gh_ready, 1)
            act.wait_ge(ld_src, 16)
            act.wait_ge(marks_ready, 1)
            nc.scalar.activation(cf[:, MIX, :], iota_b[:, :], ACT.Copy, scale=0.0).then_inc(plane_set, 1)
            act.wait_ge(plane_set, 1)
            nc.scalar.activation(cf[:, MIX, MIX:PL], ring[:, 0, ROW:RS], ACT.Copy).then_inc(plane_set, 1)
            act.wait_ge(plane_set, 2)

            def split_step(i):
                for j in range(GPS):
                    index_copy(act, CT + U * i, i, j)
                    if j == 0:
                        act.wait_ge(crow_loaded, 16 * i)
                        act.wait_ge(rest_made, i)
                        for m in range(MIX):
                            nc.scalar.activation(cf[:, m, :], crow[:, 0:D], ACT.Copy, scale=crow[:, D + m:D + m + 1])
                        nc.scalar.activation(cf[:, MIX, 0:MIX], crow[:, D:ROW], ACT.Copy).then_inc(products_made, 1)
                    if j == 1:
                        act.wait_ge(products_made, i)
                        act.wait_ge(parts_free, i)
                        nc.scalar.activation(c3[:, :, 0, :], cf, ACT.Copy).then_inc(part_hi, 1)
                    if j == 5:
                        act.wait_ge(rest_made, i + 1)
                        nc.scalar.activation(c3[:, :, 1, :], rest, ACT.Copy).then_inc(part_mid, 1)

            for j in range(GPS):
                index_copy(act, CT, 0, j)
            with act.Fori(1, S1) as i:
                split_step(i)
            split_step(S1)
            with act.Fori(1, S2) as i:
                for j in range(GPS):
                    index_copy(act, CT + U * S1 + U * i, S1 + i, j)

            def index_step(eng, i, n):
                for j in range(GPS):
                    index_copy(eng, U * i, n, j)

            general_path(act, index_step)
            act.wait_ge(edges_done, 1)
            for c in range(NCH + 2):
                if c < NCH:
                    nc.scalar.activation(acc[:, 0:MIX, cols(c)], acc[:, 0:MIX, cols(c)], ACT.Gelu).then_inc(ga_ready, 1)
                if c >= 2:
                    node_gelu(act, c - 2)

        @block.vector
        def _(v):
            link_count = [0]

            def link(ins):
                ins.then_inc(dve, 1)
                link_count[0] += 1

            def chained():
                v.wait_ge(dve, link_count[0])

            def statistics(a0, a1, part):
                v.wait_ge(ld_x[part], 16)
                for a in range(a0, a1):
                    link(nc.vector.bn_stats(stats[:, a, :], x_sb[:, a, :]))
                chained()
                for a in range(a0, a1):
                    link(nc.vector.bn_aggr(mv[:, a, :], stats[:, a, :]))
                chained()
                var, r = mv[:, a0:a1, 1], rstd[:, a0:a1]
                link(nc.vector.tensor_scalar_add(var, var, EPS))
                chained()
                link(nc.vector.tensor_scalar(r.bitcast(i32), var.bitcast(i32), 1, None, ALU.logical_shift_right))
                chained()
                link(nc.vector.tensor_scalar(r.bitcast(i32), r.bitcast(i32), -1.0, float(RSQRT_BITS),
                                             ALU.mult, ALU.add))
                for _ in range(3):
                    chained()
                    link(nc.vector.tensor_tensor(newton[:, a0:a1], r, r, ALU.mult))
                    chained()
                    link(nc.vector.scalar_tensor_tensor(newton[:, a0:a1], newton[:, a0:a1], -0.5, var,
                                                        ALU.mult, ALU.mult))
                    chained()
                    link(nc.vector.scalar_tensor_tensor(r, newton[:, a0:a1], 1.5, r, ALU.add, ALU.mult))
                chained()

            def normalise(c):
                if 4 * c in XQ:
                    statistics(XQ[x_part(c)], XQ[x_part(c) + 1], x_part(c))
                if c >= 2:
                    v.wait_ge(zt_ready, c - 1)
                for j, a in enumerate(tiles(c)):
                    last = nc.vector.tensor_scalar(z[c % 2][:, j, :], x_sb[:, a, :], mv[:, a, 0:1],
                                                   rstd[:, a:a + 1], ALU.subtract, ALU.mult)
                last.then_inc(z_ready, 1)

            normalise(0)
            for c in range(NCH + 3):
                if c + 1 < NCH:
                    normalise(c + 1)
                if c == 1:
                    v.wait_ge(ld_dstg, 16)
                    nc.vector.tensor_reduce(gmin[:, :], dstg, axis=AX.X, op=ALU.min)
                    link(nc.vector.tensor_reduce(gmax[:, :], dstg, axis=AX.X, op=ALU.max))
                    chained()
                    nc.vector.tensor_tensor(gspan[:, :], gmax[:, :], gmin[:, :], ALU.subtract)\
                        .then_inc(bounds_ready, 1)
                if c >= 3:
                    table_rows(v, c - 3)
            v.wait_ge(ld_base, 32)
            v.wait_ge(ld_dst, 16)
            v.wait_ge(ld_src, 16)
            link(nc.vector.tensor_tensor(dloc.rearrange("p (g t) -> p g t", t=G),
                                         dst_i.rearrange("p (g t) -> p g t", t=G),
                                         base_b[:, :, None].to_broadcast([P, NG, G]), ALU.subtract))
            link(nc.vector.tensor_reduce(span[:, :], spans, axis=AX.X, op=ALU.max))
            link(nc.vector.tensor_reduce(marks[:, 0:1], spans, axis=AX.X, op=ALU.max))
            link(nc.vector.tensor_reduce(marks[:, 1:2], spans[:, 0:S1 * CG], axis=AX.X, op=ALU.max))
            link(nc.vector.tensor_tensor(tops, base_b[0:1, 0:S1 * CG], spans[:, 0:S1 * CG], ALU.add))
            link(nc.vector.tensor_scalar(key_a[:, :].bitcast(i32), src_i[:, 0:CT], P.bit_length() - 1, None,
                                         ALU.logical_shift_right))
            chained()
            link(nc.vector.tensor_reduce(marks[:, 2:3], tops, axis=AX.X, op=ALU.max))
            chained()
            link(nc.vector.tensor_copy(base, base_b[0:1, :]))
            nc.vector.tensor_scalar_min(base_c, base_b[0:1, 0:S1 * CG], float(CN)).then_inc(marks_ready, 1)
            link(nc.vector.scalar_tensor_tensor(key_b[:, :], key_a[:, :].bitcast(i32), -float(P), src_i[:, 0:CT],
                                                ALU.mult, ALU.add))
            link(nc.vector.scalar_tensor_tensor(key_a[:, :], key_a[:, :].bitcast(i32), float(CW), dloc[:, 0:CT],
                                                ALU.mult, ALU.add))
            link(nc.vector.memset(acc[:, MIX - 1, :], 0.0))
            v.wait_ge(own_stored[0], 16 * ((NCH + 1) // 2))
            v.wait_ge(own_stored[1], 16 * (NCH // 2))
            link(nc.vector.memset(counts[:, :, :], 0.0))
            v.wait_ge(zeroed, 2)
            v.wait_ge(marks_ready, 1)
            chained()
            with v.Fori(0, S1) as i:
                starts = window_starts(v, start_regs_c, base_c, CG * i, CN)

                def leave_rest():
                    v.wait_ge(part_hi, i + 1)
                    nc.vector.tensor_tensor(rest, cf, c3[:, :, 0, :], ALU.subtract).then_inc(rest_made, 1)

                def last_part():
                    v.wait_ge(part_mid, i + 1)
                    v.wait_ge(rest_made, i + 2)
                    nc.vector.tensor_tensor(c3[:, :, 2, :], rest, c3[:, :, 1, :], ALU.subtract).then_inc(part_lo, 1)

                scatter_step(v, CT + U * i, S1 * CG + GPS * i, i, {
                    0: lambda: hots(v, i, 0),
                    1: lambda: hots(v, i, 1),
                    2: lambda: (add_counts(v, i, 0, starts), hots(v, i, 2)),
                    4: lambda: (leave_rest(), add_counts(v, i, 1, starts), hots(v, i, 3)),
                    5: lambda: add_counts(v, i, 2, starts),
                    6: lambda: add_counts(v, i, 3, starts),
                })
                last_part()

            def product_steps(m0, m1):
                with v.Fori(m0, m1) as m:
                    with v.Fori(0, NAB) as ab:
                        u = NAB * m + ab
                        n = S1 + u
                        if m1 == 1:
                            nc.vector.tensor_reduce(most[:, bass.ds(ab, 1)], counts[:, bass.ds(AB * ab, AB), 0:CN],
                                                    axis=AX.XY, op=ALU.max).then_inc(most_made, 1)
                        scatter_step(v, CT + U * n, S1 * CG + GPS * n, n, {})
                        v.wait_ge(multiplied, u + 2)
                        v.wait_ge(added, GPS * (n + 1) + 1)
                        at = acc[:, bass.ds(m, 1), 0:CN].rearrange("p m n -> p (m n)")
                        nc.vector.tensor_tensor(at, at, ps[:, 5, 0:CN], ALU.add).then_inc(product_added, 1)
                        v.wait_ge(product_added, u + 2)
                        v.nop(nofuse=True)

            v.wait_ge(counts_added, S1 * CG + 1)
            product_steps(0, 1)
            v.wait_ge(most_made, NAB)
            nc.vector.tensor_reduce(most_p[:, :], most[:, :], axis=AX.X, op=ALU.max).then_inc(most_ready, 1)
            product_steps(1, PL)
            v.wait_ge(most_loaded, 16)
            link(nc.vector.tensor_reduce(marks[:, 3:4], most_r, axis=AX.X, op=ALU.max))
            chained()
            for q, least in enumerate((W, CW, CN, EXACT)):
                link(nc.vector.tensor_scalar(marks[:, q:q + 1], marks[:, q:q + 1], float(least), None, ALU.is_ge))
            chained()
            nc.vector.tensor_reduce(flag[:, :], marks[:, :], axis=AX.X, op=ALU.max).then_inc(flag_ready, 1)
            v.wait_ge(flag_ready, 1)
            flagged = v.value_load(flag[0:1, 0:1], min_val=0, max_val=1)
            with v.If(flagged >= 1):
                nc.vector.memset(acc[:, 0:MIX, :], 0.0).then_inc(cleared, 1)
                nc.vector.memset(accs, 0.0).then_inc(cleared, 1)
                v.wait_ge(cleared, 2)
                widest = v.value_load(span[0:1, 0:1], min_val=0, max_val=N)
                with v.Fori(0, PASSES) as q:
                    with v.If(widest >= q * W):
                        with v.Fori(0, STEPS) as i:
                            scatter_step(v, U * i, GPS * i, S1 + S2 + q * STEPS + i, {})
                        nc.vector.tensor_scalar(base, base, float(W), float(N), ALU.add, ALU.min).then_inc(moved, 1)
                        nc.vector.tensor_scalar_add(iota[:, :, :], iota[:, :, :], float(W)).then_inc(moved, 1)
                        v.wait_ge(moved, 2 * q + 2)
                        v.nop(nofuse=True)
            nc.vector.memset(done[:, :], 0.0).then_inc(edges_done, 1)
            v.wait_ge(sums_loaded, 16)
            count = sums_n[:, MIX, :]
            link(nc.vector.tensor_scalar_max(count, count, 1.0))
            chained()
            link(nc.vector.reciprocal(count, count))
            chained()
            nc.vector.tensor_tensor(weights_n, sums_n[:, 0:MIX, :],
                                    count[:, None, :].to_broadcast([P, MIX, NT]), ALU.mult).then_inc(weights_ready, 1)
            for c in range(NCH + 3):
                if c < NCH:
                    k = P * len(tiles(c))
                    v.wait_ge(ga_ready, c + 1)
                    v.wait_ge(spread_loaded[c % 3], 16 * (c // 3 + 1))
                    nc.vector.tensor_tensor(acc[:, 0:MIX, cols(c)], acc[:, 0:MIX, cols(c)], spread[c % 3][:, :, 0:k],
                                            ALU.mult).then_inc(prod_ready, 1)
                if 1 <= c < NCH + 1:
                    v.wait_ge(pair_ready, c)
                    nc.vector.tensor_tensor(acc[:, 0, cols(c - 1)], acc[:, 0, cols(c - 1)], acc[:, 1, cols(c - 1)],
                                            ALU.add).then_inc(node_ready, 1)
                if c >= 3:
                    results(v, c - 3)

        @block.tensor
        def _(pe):
            pe.wait_ge(consts, 7)
            pe.wait_ge(ld_w, 96)
            for c in range(NCH + 3):
                if c < NCH:
                    pe.wait_ge(z_ready, c + 1)
                    if c >= 2:
                        pe.wait_ge(hn_ready, c - 1)
                    for j in range(len(tiles(c))):
                        last = nc.tensor.transpose(ps[:, c % 2, P * j:P * j + P], z[c % 2][:, j, :], ident)
                    last.then_inc(zt_ready, 1)
                if 1 <= c < NCH + 1:
                    b = c - 1
                    k = P * len(tiles(b))
                    pe.wait_ge(hn_ready, b + 1)
                    if b >= 1:
                        pe.wait_ge(ht_ready, b)
                    nc.tensor.matmul(ps[:, 2, 0:k], w1_sb, hn[b % 2][:, 0:k], start=True, stop=True)\
                        .then_inc(h_ready, 1)
                if 2 <= c < NCH + 2:
                    b = c - 2
                    k = P * len(tiles(b))
                    pe.wait_ge(ht_ready, b + 1)
                    if b >= 1:
                        pe.wait_ge(gu_ready, b)
                    nc.tensor.matmul(ps[:, 3, 0:k], wa_sb, ht[b % 3][:, 0:k], start=True, stop=True)\
                        .then_inc(u_ready, 1)
                if c >= 3:
                    node_rows(pe, c - 3)
            for q in range(MS):
                last = nc.tensor.matmul(ps[:, q, MIX * W:PL * W], zero[:, :], zero[:, 0:W], start=True, stop=True)
            with pe.Fori(0, S1) as i:
                sum_step(pe, i, {1: lambda: count(pe, i, 0), 2: lambda: count(pe, i, 1),
                                 3: lambda: count(pe, i, 2), 5: lambda: count(pe, i, 3)})

            pe.wait_ge(counts_added, S1 * CG + 1)
            with pe.Fori(0, PL) as m:
                with pe.Fori(0, NAB) as ab:
                    u = NAB * m + ab

                    def multiply(a):
                        if a == 0:
                            pe.wait_ge(cbuf_loaded, 16 * u + 16)
                            pe.wait_ge(product_added, u + 1)
                        for part in range(SPL):
                            last = nc.tensor.matmul(
                                ps[:, 5, 0:CN], cbuf[:, a, part, :],
                                counts[:, bass.ds(AB * ab + a, 1), 0:CN].rearrange("p a n -> p (a n)"),
                                start=(a == 0 and part == 0), stop=(a == AB - 1 and part == SPL - 1))
                        if a == AB - 1:
                            last.then_inc(multiplied, 1)

                    sum_step(pe, S1 + u, {a: partial(multiply, a) for a in range(AB)})
            general_path(pe, lambda eng, i, n: sum_step(eng, n, {}))
            for c in range(NCH):
                project(pe, c)


_OUT = "out_dram"


def kernel(x, src, dst, L0_gnn_W1, L0_gnn_b1, L0_gnn_WA, L0_gnn_WB, L0_gnn_W2, L0_gnn_b2):
    import numpy as _np
    import concourse.bacc as _bacc
    from concourse import mybir as _mybir
    from concourse.bass_utils import run_bass_kernel_spmd as _run

    def by_partition(a):
        return _np.ascontiguousarray(a.reshape(-1, P, *a.shape[1:]).swapaxes(0, 1))

    x, src, dst = _np.asarray(x), _np.asarray(src), _np.asarray(dst)
    w2 = _np.asarray(L0_gnn_W2)
    pad = ET * P - E
    laid_out = {
        "x": by_partition(_np.pad(x, ((0, NT * P - N), (0, 0)))),
        "src_by_edge": by_partition(_np.pad(src, (0, pad))),
        "dst_by_edge": by_partition(_np.pad(dst, (0, pad), constant_values=PAD_DST)),
        "dst_by_group": _np.pad(dst, (0, pad), mode="edge").reshape(GP, GC, G * P),
        "W1t": _np.asarray(L0_gnn_W1).T,
        "b1": _np.asarray(L0_gnn_b1).reshape(D, 1),
        "WAt": _np.asarray(L0_gnn_WA).T,
        "WBt": _np.asarray(L0_gnn_WB).T,
        "W2t": w2.T.reshape(2, D, D).swapaxes(0, 1),
        "b2": _np.asarray(L0_gnn_b2).reshape(1, D),
    }
    nc = _bacc.Bacc("TRN2", target_bir_lowering=False, num_devices=1)
    arrays, args = {}, []
    for name, a in laid_out.items():
        arrays[f"in_{name}"] = a = _np.ascontiguousarray(a)
        args.append(nc.dram_tensor(f"in_{name}", a.shape, _mybir.dt.from_np(a.dtype), kind="ExternalInput").ap())
    out = nc.dram_tensor(_OUT, (P, NT, D), _mybir.dt.float32, kind="ExternalOutput").ap()
    gnn_kernel(nc, *args, out)
    r = _run(nc, [arrays], core_ids=[0])
    return r.results[0][_OUT].swapaxes(0, 1).reshape(NT * P, D)[:N]
```

```python
import concourse.bass as bass
from concourse import mybir
from contextlib import ExitStack
from functools import partial

P = 128
N = 6250
E = 200000
D = 128
MIX = 4
NT = -(-N // P)
NCH = -(-NT // 4)
EARLY = 10
AHEAD = 6
G = 2
GPS = 7
U = GPS * G
STEPS = -(-E // (P * U))
ET = STEPS * U
NG = ET // G
GP = 112
GC = NG // GP
W = 24
PASSES = -(-N // W)
NACC = N + W
MS = 3
ROW = D + MIX
RS = ROW + 1
PAD_DST = 1 << 20
CG = 4
CT = NT * CG * G
CN = 416
CW = 8
AW = CN + CW
PL = MIX + 1
SPL = 3
WROWS = MIX * SPL
EXACT = 256
AB = 7
NAB = NT // AB
S1 = NT
S2 = PL * NAB
assert CT + (S1 + S2) * U == ET and NAB * AB == NT and AB <= GPS
EPS = 1e-5
RSQRT_BITS = 0x5F3759DF
assert NG == GP * GC and NACC >= NT * P


def gnn_kernel(nc, x, src_e, dst_e, dst_g, w1t, b1, wat, wbt, w2t, b2, out):
    f32 = mybir.dt.float32
    i32 = mybir.dt.int32
    i16 = mybir.dt.int16
    bf16 = mybir.dt.bfloat16
    f16 = mybir.dt.float16
    ALU = mybir.AluOpType
    ACT = mybir.ActivationFunctionType
    AX = mybir.AxisListType

    ctx = ExitStack()
    with ctx:
        def sb(name, shape, dt=f32):
            return ctx.enter_context(nc.sbuf_tensor(name, shape, dt))

        def sem(name):
            return ctx.enter_context(nc.semaphore(name))

        table = nc.dram_tensor("node_table", [NT * P, ROW], f32, kind="Internal").ap()
        parts = nc.dram_tensor("product_parts", [PL, NT, P, SPL * P], bf16, kind="Internal").ap()
        own = nc.dram_tensor("own_part", [P, NT, D], f32, kind="Internal").ap()
        most_d = nc.dram_tensor("largest_counts", [P], f32, kind="Internal").ap()
        sums_d = nc.dram_tensor("mix_sums", [MIX + 1, NT * P], f32, kind="Internal").ap()
        weights_d = nc.dram_tensor("mix_weights", [WROWS, NT * P], bf16, kind="Internal").ap()
        bounds = nc.dram_tensor("window_bounds", [2, NG], i32, kind="Internal").ap()

        counts = sb("counts", [P, NT, AW], bf16)
        x_sb = counts[:, :, :].rearrange("p a n -> p (a n)").bitcast(f32)[:, 0:NT * D]\
            .rearrange("p (a d) -> p a d", d=D)
        words = counts[:, :, :].rearrange("p a n -> p (a n)").bitcast(f32)

        def behind_x(at, size):
            return words[:, NT * D + at:NT * D + at + size]

        ident = behind_x(0, P)
        w1_sb = behind_x(P, D)
        wa_sb = behind_x(P + D, D)
        w2b_sb = behind_x(P + 2 * D, D)
        b2_sb = behind_x(P + 3 * D, D)
        rstd = behind_x(P + 4 * D, NT)
        mv = behind_x(P + 4 * D + NT, 2 * NT).rearrange("p (a s) -> p a s", s=2)
        weights = behind_x(0, NT * P // 2).bitcast(bf16)[0:WROWS, :]
        sums_n = behind_x(NT * P // 2, PL * NT).rearrange("p (m a) -> p m a", m=PL)
        acc = sb("acc", [P, PL, NACC])
        accs = acc[0:PL, MIX, :]
        edges = sb("edges", [P, 2, ET], i32)
        src_i, dst_i = edges[:, 0, :], edges[:, 1, :]
        dloc = dst_i.bitcast(f32)
        gmin = sb("gmin", [GP, GC], i32)
        gmax = sb("gmax", [GP, GC], i32)
        gspan = sb("gspan", [GP, GC], i32)
        key_a = sb("key_a", [P, CT])
        key_b = sb("key_b", [P, CT])
        zero = sb("zero", [P, P], bf16)
        iota_a = sb("iota_a", [P, NT * CW], f16)
        iota_b = sb("iota_b", [P, P], bf16)
        hot_a = sb("hot_a", [P, 2, G, NT * CW], bf16)
        choose = hot_a[0:WROWS, :, :, :].rearrange("p b t n -> p (b t n)")[:, 0:MIX * P]\
            .rearrange("p (m n) -> p m n", m=MIX)
        hot_b = sb("hot_b", [P, 2, G, P], bf16)
        most = sb("most", [P, NAB])
        most_p = sb("most_p", [P, 1])
        marks = sb("marks", [1, 4])
        flag = sb("flag", [1, 1], i32)
        span = sb("span", [1, 1], i32)
        idx = sb("idx", [P, U], i32)
        ring = sb("ring", [P, U, RS])
        mask = sb("mask", [P, MS, G, MIX + 1, W])
        iota = sb("iota", [P, MIX + 1, W])
        wb_sb = sb("wb_sb", [P, MIX])
        w2a_sb = sb("w2a_sb", [P, D])
        b1_sb = sb("b1_sb", [P, 1])
        done = sb("done", [P, 1])
        row = sb("row", [P, 2, 4, ROW])
        work = acc[:, MIX - 1, 0:12 * 4 * P].rearrange("p (k n) -> p k n", k=12)
        z = [work[:, i, :].rearrange("p (a d) -> p a d", d=D) for i in (0, 1)]
        hn = [work[:, i, :] for i in (2, 3)]
        ht = [work[:, i, :] for i in (4, 5, 6)]
        gu = [work[:, i, :] for i in (7, 8)]
        gh = [work[:, i, :] for i in (9, 10)]
        stats = work[:, 11, 0:6 * NT].rearrange("p (a s) -> p a s", s=6)
        newton = work[:, 11, 6 * NT:7 * NT]
        room = sb("room", [P, MIX * 4 * P])
        dstg = room[0:GP, 0:GC * G * P].bitcast(i32).rearrange("p (c e) -> p c e", c=GC)
        base_b = room[:, 0:NG].bitcast(i32)
        spans = room[0:1, NG:2 * NG].bitcast(i32)
        tops = room[0:1, 2 * NG:2 * NG + S1 * CG]
        cf = room[:, 0:PL * P].rearrange("p (m d) -> p m d", m=PL)
        rest = room[:, PL * P:2 * PL * P].rearrange("p (m d) -> p m d", m=PL)
        crow = room[:, 2 * PL * P:2 * PL * P + ROW]
        most_r = room[0:1, 2 * PL * P + ROW:2 * PL * P + ROW + P]
        c3 = row[:, :, :, :].rearrange("p b a d -> p (b a d)").bitcast(bf16)[:, 0:PL * SPL * P]\
            .rearrange("p (m s d) -> p m s d", m=PL, s=SPL)
        after_most = 2 * PL * P + ROW + P
        base = room[0:1, after_most:after_most + NG // 2].bitcast(i16)
        base_c = room[0:1, after_most + NG // 2:after_most + (NG + S1 * CG) // 2].bitcast(i16)
        cbuf = room[:, :].bitcast(bf16)[:, 0:AB * SPL * P].rearrange("p (a s d) -> p a s d", a=AB, s=SPL)
        res = room[:, 0:8 * D].rearrange("p (b a d) -> p b a d", b=2, a=4)
        weights_n = room[:, 8 * D:8 * D + MIX * NT].rearrange("p (m a) -> p m a", m=MIX)
        left_n = room[:, 10 * D:10 * D + MIX * NT].rearrange("p (m a) -> p m a", m=MIX)
        parts_n = room[:, 12 * D:12 * D + WROWS * NT // 2].bitcast(bf16)\
            .rearrange("p (m s a) -> p m s a", m=MIX, s=SPL)
        unit = room[:, 15 * D:16 * D]
        fa = [row[:, i, :, :].rearrange("p a d -> p (a d)") for i in (0, 1)]
        ps = ctx.enter_context(nc.psum_tensor("ps", [P, 8, 512], f32))

        XQ = [0, 4, 12, 20, 28, 36, 44, NT]
        XP = len(XQ) - 1
        ld_x = [sem(f"ld_x{i}") for i in range(XP)]
        ld_w = sem("ld_w")
        ld_b2 = sem("ld_b2")
        ld_src = sem("ld_src")
        ld_dst = sem("ld_dst")
        ld_dstg = sem("ld_dstg")
        consts = sem("consts")
        zeroed = sem("zeroed")
        chosen = sem("chosen")
        dve = sem("dve_chain")
        st_bounds = sem("st_bounds")
        ld_base = sem("ld_base")
        b2_added = sem("b2_added")
        bounds_ready = sem("bounds_ready")
        z_ready = sem("z_ready")
        zt_ready = sem("zt_ready")
        hn_ready = sem("hn_ready")
        stats_ready = sem("stats_ready")
        h_ready = sem("h_ready")
        ht_ready = sem("ht_ready")
        u_ready = sem("u_ready")
        gu_ready = sem("gu_ready")
        rows_ready = sem("rows_ready")
        t_copied = sem("t_copied")
        h_copied = sem("h_copied")
        row_stored = [sem(f"row_stored{i}") for i in range(2)]
        idx_ready = sem("idx_ready")
        gathered = [sem(f"gathered{i}") for i in range(U)]
        masks_ready = sem("masks_ready")
        group_summed = sem("group_summed")
        added = sem("added")
        own_stored = [sem(f"own_stored{i}") for i in range(2)]
        own_loaded = [sem(f"own_loaded{i}") for i in range(4)]
        marks_ready = sem("marks_ready")
        plane_set = sem("plane_set")
        hots_ready = sem("hots_ready")
        counted = sem("counted")
        counts_added = sem("counts_added")
        crow_loaded = sem("crow_loaded")
        products_made = sem("products_made")
        part_hi = sem("part_hi")
        rest_made = sem("rest_made")
        part_mid = sem("part_mid")
        part_lo = sem("part_lo")
        parts_stored = sem("parts_stored")
        parts_free = sem("parts_free")
        cbuf_loaded = sem("cbuf_loaded")
        multiplied = sem("multiplied")
        product_added = sem("product_added")
        most_made = sem("most_made")
        most_ready = sem("most_ready")
        most_stored = sem("most_stored")
        most_loaded = sem("most_loaded")
        moved = sem("moved")
        cleared = sem("cleared")
        flag_ready = sem("flag_ready")
        edges_done = sem("edges_done")
        own_ready = sem("own_ready")
        own_added = sem("own_added")
        gh_ready = sem("gh_ready")
        ga_ready = sem("ga_ready")
        sums_stored = sem("sums_stored")
        sums_loaded = sem("sums_loaded")
        weights_ready = sem("weights_ready")
        weights_stored = sem("weights_stored")
        weights_loaded = sem("weights_loaded")
        spread = sem("spread")
        prod_ready = sem("prod_ready")
        pair_ready = sem("pair_ready")
        node_ready = sem("node_ready")
        fa_ready = sem("fa_ready")
        out_ready = sem("out_ready")
        res_ready = sem("res_ready")
        res_stored = [sem(f"res_stored{i}") for i in range(2)]

        block = ctx.enter_context(nc.Block())

        def tiles(c):
            return range(4 * c, min(4 * c + 4, NT))

        def cols(c):
            return slice(512 * c, 512 * c + P * len(tiles(c)))


        def x_part(c):
            return next(q for q in range(XP) if 4 * c < XQ[q + 1])


        def gather_step(pool, n):
            for j in range(GPS):
                pool.wait_ge(idx_ready, GPS * n + j + 1)
                pool.nop(nofuse=True)
                for s in range(G * j, G * j + G):
                    pool.indirect_dma_start(
                        out=ring[:, s, 0:ROW], out_offset=None, in_=table,
                        in_offset=bass.IndirectOffsetOnAxis(ap=idx[:, s:s + 1], axis=0),
                    ).then_inc(gathered[s], 16)

        def index_copy(act, tile, n, j):
            act.wait_ge(group_summed, GPS * n + j + 1)
            nc.scalar.activation(idx[:, G * j:G * j + G], src_i[:, bass.ds(tile + G * j, G)],
                                 ACT.Copy).then_inc(idx_ready, 1)

        def h_rows(act, c):
            k = len(tiles(c))
            act.wait_ge(rows_ready, c + 1)
            if c >= 2:
                act.wait_ge(row_stored[c % 2], 16 * (c // 2))
            nc.scalar.activation(row[:, c % 2, 0:k, 0:D],
                                 ps[:, 4 + c % 2, 0:P * k].rearrange("p (a d) -> p a d", d=D),
                                 ACT.Copy).then_inc(h_copied, 1)

        def node_gelu(act, c):
            k = P * len(tiles(c))
            act.wait_ge(node_ready, c + 1)
            if c >= 2:
                act.wait_ge(out_ready, c - 1)
            nc.scalar.activation(fa[c % 2][:, 0:k], acc[:, 0, cols(c)], ACT.Gelu).then_inc(fa_ready, 1)

        def results(act, c):
            k = len(tiles(c))
            act.wait_ge(out_ready, c + 1)
            if c >= 2:
                act.wait_ge(res_stored[c % 2], 16 * (c // 2))
            nc.scalar.activation(res[:, c % 2, 0:k, :], ps[:, 6 + c % 2, 0:P * k].rearrange("p (a d) -> p a d", d=D),
                                 ACT.Copy).then_inc(res_ready, 1)

        def table_rows(v, c):
            k = len(tiles(c))
            v.wait_ge(rows_ready, c + 1)
            if c >= 2:
                v.wait_ge(row_stored[c % 2], 16 * (c // 2))
            nc.vector.tensor_copy(row[:, c % 2, 0:k, D:ROW],
                                  ps[:, 6, 0:MIX * k].rearrange("p (a m) -> p a m", m=MIX))\
                .then_inc(t_copied, 1)
            v.wait_ge(own_ready, c + 1)
            v.wait_ge(b2_added, c + 1)
            nc.vector.tensor_tensor(x_sb[:, 4 * c:4 * c + k, :], x_sb[:, 4 * c:4 * c + k, :],
                                    ps[:, 7, 0:P * k].rearrange("p (a d) -> p a d", d=D),
                                    ALU.add).then_inc(own_added, 1)

        def window_starts(v, regs, row, first, largest):
            v.load(regs, row[:, bass.ds(first, len(regs))])
            return [v.snap(reg, min_val=0, max_val=largest) for reg in regs]

        start_regs = [nc.vector.alloc_register(f"start_{j}") for j in range(GPS)]
        start_regs_c = [nc.vector.alloc_register(f"start_in_a_{g}") for g in range(CG)]

        def scatter_step(v, tile, group, n, between):
            def masks(j):
                for t in range(G):
                    s = G * j + t
                    v.wait_ge(gathered[s], 16 * n + 16)
                    last = nc.vector.scalar_tensor_tensor(
                        mask[:, j % MS, t, :, :], iota[:, :, :], dloc[:, bass.ds(tile + s, 1)],
                        ring[:, s, D:D + MIX + 1][:, :, None].to_broadcast([P, MIX + 1, W]),
                        ALU.is_equal, ALU.mult)
                last.then_inc(masks_ready, 1)

            starts = window_starts(v, start_regs, base, group, N)

            def add(j):
                v.wait_ge(group_summed, GPS * n + GPS + j + 1)
                v.wait_ge(added, GPS * n + j + 1)
                at = acc[:, :, bass.ds(starts[j], W)]
                nc.vector.tensor_tensor(at, at, ps[:, j % MS, 0:PL * W].rearrange("p (m w) -> p m w", w=W),
                                        ALU.add).then_inc(added, 1)

            for j in range(GPS):
                masks(j)
                if j >= MS - 1:
                    add(j - MS + 1)
                if j in between:
                    between[j]()
            for j in range(GPS - MS + 1, GPS):
                add(j)

        def hots(v, i, g):
            for t in range(G):
                at = bass.ds(G * (CG * i + g) + t, 1)
                nc.vector.tensor_scalar(hot_b[:, g % 2, t, :], iota_b[:, :], key_b[:, at], None, ALU.is_equal)
                last = nc.vector.tensor_scalar(hot_a[:, g % 2, t, :], iota_a[:, :], key_a[:, at], None, ALU.is_equal)
            last.then_inc(hots_ready, 1)

        def add_counts(v, i, g, starts):
            v.wait_ge(counted, CG * i + g + 1)
            v.wait_ge(counts_added, CG * i + g + 1)
            at = counts[:, :, bass.ds(starts[g], CW)]
            nc.vector.tensor_tensor(at, at, ps[:, 3 + g % 2, 0:NT * CW].rearrange("p (a w) -> p a w", w=CW),
                                    ALU.add).then_inc(counts_added, 1)

        def project(pe, c):
            pe.wait_ge(own_loaded[c // 4], 16)
            if c >= 2:
                pe.wait_ge(res_ready, c - 1)
            k = len(tiles(c))
            nc.tensor.matmul(ps[:, 6 + c % 2, 0:P * k], unit, x_sb[:, 4 * c:4 * c + k, :].rearrange("p a d -> p (a d)"),
                             start=True, stop=False)
            pe.wait_ge(fa_ready, c + 1)
            for j in range(k):
                o = ps[:, 6 + c % 2, P * j:P * j + P]
                last = nc.tensor.matmul(o, fa[c % 2][:, P * j:P * j + P], w2a_sb[:, :], start=False, stop=(j == k - 1))
            last.then_inc(out_ready, 1)

        def spread_weights(pe, c, h):
            t = 2 * c + h
            if t >= 3:
                pe.wait_ge(prod_ready, t - 2)
            for b in range(2):
                last = nc.tensor.matmul(ps[:, 2 * (t % 3) + b, 0:P * len(tiles(c))], choose[:, 2 * h + b, :],
                                        weights[:, P * 4 * c:P * 4 * c + P * len(tiles(c))], start=True, stop=True)
            last.then_inc(spread, 1)

        def node_rows(pe, c):
            if c >= 2:
                pe.wait_ge(h_copied, c - 1)
            pe.wait_ge(gu_ready, c + 1)
            for j in range(len(tiles(c))):
                nc.tensor.transpose(ps[:, 4 + c % 2, P * j:P * j + P], ht[c % 3][:, P * j:P * j + P], ident)
            if c > 0:
                pe.wait_ge(t_copied, c)
            for j in range(len(tiles(c))):
                m = MIX * j
                last = nc.tensor.matmul(ps[:, 6, m:m + MIX], gu[c % 2][:, P * j:P * j + P],
                                        wb_sb[:, :], start=True, stop=True)
            last.then_inc(rows_ready, 1)
            if c > 0:
                pe.wait_ge(own_added, c)
            pe.wait_ge(gh_ready, c + 1)
            for j in range(len(tiles(c))):
                last = nc.tensor.matmul(ps[:, 7, P * j:P * j + P], gh[c % 2][:, P * j:P * j + P], w2b_sb,
                                        start=True, stop=True)
            last.then_inc(own_ready, 1)

        def sum_step(pe, n, between):
            for j in range(GPS):
                pe.wait_ge(masks_ready, GPS * n + j + 1)
                o = ps[:, j % MS, :]
                for t in range(G):
                    nc.tensor.matmul(o[:, 0:MIX * W], ring[:, G * j + t, 0:D],
                                     mask[:, j % MS, t, 0:MIX, :], start=(t == 0), stop=(t == G - 1))
                for t in range(G):
                    last = nc.tensor.matmul(o[0:PL, MIX * W:(MIX + 1) * W], ring[:, G * j + t, D:RS],
                                            mask[:, j % MS, t, MIX, :], start=(t == 0), stop=(t == G - 1))
                last.then_inc(group_summed, 1)
                if j in between:
                    between[j]()

        def count(pe, i, g):
            pe.wait_ge(hots_ready, CG * i + g + 1)
            for t in range(G):
                last = nc.tensor.matmul(ps[:, 3 + g % 2, 0:NT * CW], hot_b[:, g % 2, t, :], hot_a[:, g % 2, t, :],
                                        start=(t == 0), stop=(t == G - 1))
            last.then_inc(counted, 1)

        def general_path(eng, step):
            eng.wait_ge(flag_ready, 1)
            flagged = eng.value_load(flag[0:1, 0:1], min_val=0, max_val=1)
            with eng.If(flagged >= 1):
                widest = eng.value_load(span[0:1, 0:1], min_val=0, max_val=N)
                with eng.Fori(0, PASSES) as q:
                    with eng.If(widest >= q * W):
                        with eng.Fori(0, STEPS) as i:
                            step(eng, i, S1 + S2 + q * STEPS + i)

        def table_stored(eng):
            eng.wait_ge(row_stored[0], 16 * ((NCH + 1) // 2))
            eng.wait_ge(row_stored[1], 16 * (NCH // 2))

        def load_parts(sp_, m0, m1):
            with sp_.Fori(m0, m1) as m:
                with sp_.Fori(0, NAB) as ab:
                    sp_.wait_ge(multiplied, NAB * m + ab + 1)
                    sp_.dma_start(cbuf.rearrange("p a s d -> p a (s d)"),
                                  parts[bass.ds(m, 1), bass.ds(AB * ab, AB), :, :]
                                  .rearrange("m a p x -> p (m a) x")).then_inc(cbuf_loaded, 16)

        def store(sp_, c):
            k = len(tiles(c))
            sp_.wait_ge(res_ready, c + 1)
            sp_.dma_start(out[:, 4 * c:4 * c + k, :], res[:, c % 2, 0:k, :]).then_inc(res_stored[c % 2], 16)

        @block.sync
        def _(sp_):
            sp_.dma_start(x_sb[:, XQ[0]:XQ[1], :], x[:, XQ[0]:XQ[1], :]).then_inc(ld_x[0], 16)
            sp_.dma_start(x_sb[:, XQ[1]:XQ[2], :], x[:, XQ[1]:XQ[2], :]).then_inc(ld_x[1], 16)
            for t, a in ((w1_sb, w1t), (wa_sb, wat), (wb_sb[:, :], wbt)):
                sp_.dma_start(t, a).then_inc(ld_w, 16)
            sp_.dma_start(w2a_sb[:, :], w2t[:, 0, :]).then_inc(ld_w, 16)
            sp_.dma_start(w2b_sb, w2t[:, 1, :]).then_inc(ld_w, 16)
            sp_.dma_start(b1_sb[:, :], b1).then_inc(ld_w, 16)
            sp_.dma_start(b2_sb, b2.to_broadcast([P, D])).then_inc(ld_b2, 16)
            sp_.dma_start(dstg, dst_g).then_inc(ld_dstg, 16)
            for q in range(2, XP):
                sp_.dma_start(x_sb[:, XQ[q]:XQ[q + 1], :], x[:, XQ[q]:XQ[q + 1], :]).then_inc(ld_x[q], 16)
            sp_.dma_start(dst_i, dst_e).then_inc(ld_dst, 16)
            sp_.dma_start(src_i, src_e).then_inc(ld_src, 16)
            sp_.wait_ge(bounds_ready, 1)
            sp_.dma_start(bounds[0, :].rearrange("(p c) -> p c", c=GC), gmin[:, :]).then_inc(st_bounds, 16)
            sp_.dma_start(bounds[1, :].rearrange("(p c) -> p c", c=GC), gspan[:, :]).then_inc(st_bounds, 16)
            sp_.wait_ge(st_bounds, 32)
            sp_.dma_start(base_b, bounds[0:1, :].to_broadcast([P, NG])).then_inc(ld_base, 16)
            sp_.dma_start(spans, bounds[1:2, :]).then_inc(ld_base, 16)
            for c in range(NCH):
                k = len(tiles(c))
                sp_.wait_ge(h_copied, c + 1)
                sp_.wait_ge(t_copied, c + 1)
                sp_.dma_start(table[cols(c), :].rearrange("(a p) d -> p a d", p=P),
                              row[:, c % 2, 0:k, :]).then_inc(row_stored[c % 2], 16)
                sp_.wait_ge(own_added, c + 1)
                sp_.dma_start(own[:, 4 * c:4 * c + k, :], x_sb[:, 4 * c:4 * c + k, :])\
                    .then_inc(own_stored[c >= EARLY], 16)
            sp_.sem_inc(parts_free, 1)
            table_stored(sp_)
            sp_.wait_ge(marks_ready, 1)
            sp_.dma_start(crow, table[0:P, :]).then_inc(crow_loaded, 16)
            with sp_.Fori(1, NT) as i:
                sp_.wait_ge(products_made, i)
                sp_.dma_start(crow, table[bass.ds(P * i, P), :]).then_inc(crow_loaded, 16)
                sp_.wait_ge(part_lo, i)
                sp_.dma_start(parts[:, bass.ds(i - 1, 1), :, :].rearrange("m a p x -> p (m a) x"),
                              c3.rearrange("p m s d -> p m (s d)")).then_inc(parts_stored, 16)
                sp_.wait_ge(parts_stored, 16 * i)
                sp_.sem_inc(parts_free, 1)
            sp_.wait_ge(part_lo, NT)
            sp_.dma_start(parts[:, NT - 1, :, :].rearrange("m p x -> p m x"),
                          c3.rearrange("p m s d -> p m (s d)")).then_inc(parts_stored, 16)
            sp_.wait_ge(parts_stored, 16 * NT)
            load_parts(sp_, 0, 1)
            sp_.wait_ge(most_ready, 1)
            sp_.dma_start(most_d.rearrange("(p a) -> p a", a=1), most_p[:, :]).then_inc(most_stored, 16)
            sp_.wait_ge(most_stored, 16)
            sp_.dma_start(most_r, most_d.rearrange("(a p) -> a p", a=1)).then_inc(most_loaded, 16)
            load_parts(sp_, 1, PL)
            sp_.wait_ge(edges_done, 1)
            sp_.wait_ge(multiplied, S2 + 1)
            sp_.dma_start(sums_d, accs[:, 0:NT * P]).then_inc(sums_stored, 16)
            sp_.wait_ge(sums_stored, 16)
            sp_.dma_start(sums_n, sums_d.rearrange("r (p a) -> p r a", a=NT)).then_inc(sums_loaded, 16)
            sp_.wait_ge(weights_ready, 1)
            sp_.dma_start(weights_d.rearrange("r (p a) -> p r a", a=NT),
                          parts_n.rearrange("p m s a -> p (m s) a")).then_inc(weights_stored, 16)
            sp_.wait_ge(weights_stored, 16)
            sp_.dma_start(weights, weights_d).then_inc(weights_loaded, 16)
            for q in range(4):
                a = slice(16 * q, min(16 * q + 16, NT))
                sp_.dma_start(x_sb[:, a, :], own[:, a, :]).then_inc(own_loaded[q], 16)
            for c in range(NCH):
                store(sp_, c)
            sp_.wait_ge(res_stored[0], 16 * ((NCH + 1) // 2))
            sp_.wait_ge(res_stored[1], 16 * (NCH // 2))

        @block.gpsimd
        def _(pool):
            pool.memset(ident, 0.0).then_inc(consts, 1)
            pool.iota(iota[:, :, :], [[0, MIX + 1], [1, W]], base=0, channel_multiplier=0,
                      allow_small_or_imprecise_dtypes=True).then_inc(consts, 1)
            pool.iota(iota_a[:, :], [[1, NT * CW]], base=0, channel_multiplier=0,
                      allow_small_or_imprecise_dtypes=True).then_inc(consts, 1)
            pool.iota(iota_b[:, :], [[1, P]], base=0, channel_multiplier=0,
                      allow_small_or_imprecise_dtypes=True).then_inc(consts, 1)
            pool.wait_ge(consts, 4)
            pool.affine_select(out=ident, in_=ident, compare_op=ALU.not_equal, fill=1.0,
                               base=0, pattern=[[-1, P]], channel_multiplier=1).then_inc(consts, 1)
            pool.memset(ring[:, :, ROW:RS], 1.0).then_inc(consts, 1)
            pool.memset(zero[:, :], 0.0).then_inc(consts, 1)

            clear = [acc[:, m, NACC * q // 3:NACC * (q + 1) // 3] for m in (*range(MIX - 1), MIX) for q in range(3)]
            assert len(clear) == NCH - 1
            for c in range(NCH):
                if c == 0:
                    pool.wait_ge(ld_b2, 16)
                else:
                    pool.memset(clear[c - 1], 0.0).then_inc(zeroed, 1)
                k = len(tiles(c))
                pool.wait_ge(z_ready, c + 1)
                pool.tensor_tensor(x_sb[:, 4 * c:4 * c + k, :], x_sb[:, 4 * c:4 * c + k, :],
                                   b2_sb[:, None, :].to_broadcast([P, k, D]), ALU.add).then_inc(b2_added, 1)
            pool.wait_ge(own_stored[0], 16 * EARLY)
            pool.memset(words[:, 0:4 * EARLY * D], 0.0).then_inc(zeroed, 1)
            pool.sem_inc(group_summed, GPS)
            for first in (added, counts_added, rest_made, multiplied, product_added):
                pool.sem_inc(first, 1)
            table_stored(pool)
            with pool.Fori(0, S1 + S2) as i:
                gather_step(pool, i)
            general_path(pool, lambda eng, i, n: gather_step(eng, n))
            pool.wait_ge(edges_done, 1)
            pool.memset(unit, 0.0).then_inc(chosen, 1)
            pool.memset(choose[:, :, :], 1.0).then_inc(chosen, 1)
            pool.wait_ge(chosen, 2)
            pool.affine_select(out=unit, in_=unit, compare_op=ALU.not_equal, fill=1.0,
                               base=0, pattern=[[-1, P]], channel_multiplier=1).then_inc(chosen, 1)
            pool.affine_select(out=choose[:, :, :], in_=choose[:, :, :], compare_op=ALU.is_ge, fill=0.0,
                               base=0, pattern=[[-SPL, MIX], [0, P]], channel_multiplier=1).then_inc(chosen, 1)
            pool.wait_ge(chosen, 4)
            pool.affine_select(out=choose[:, :, :], in_=choose[:, :, :], compare_op=ALU.is_ge, fill=0.0,
                               base=SPL - 1, pattern=[[SPL, MIX], [0, P]], channel_multiplier=-1).then_inc(chosen, 1)
            for c in range(NCH):
                pool.wait_ge(prod_ready, 2 * c + 2)
                pool.tensor_tensor(acc[:, 0:2, cols(c)], acc[:, 0:2, cols(c)], acc[:, 2:4, cols(c)],
                                   ALU.add).then_inc(pair_ready, 1)

        @block.scalar
        def _(act):

            def normalise(c):
                act.wait_ge(stats_ready, x_part(c) + 1)
                if c >= 2:
                    act.wait_ge(zt_ready, c - 1)
                for j, a in enumerate(tiles(c)):
                    last = nc.scalar.activation(z[c % 2][:, j, :], x_sb[:, a, :], ACT.Identity,
                                                scale=rstd[:, a:a + 1], bias=mv[:, a, 0:1])
                last.then_inc(z_ready, 1)

            normalise(0)
            act.wait_ge(ld_w, 96)
            for c in range(NCH + 3):
                if c + 1 < NCH:
                    normalise(c + 1)
                if c < NCH:
                    k = P * len(tiles(c))
                    act.wait_ge(zt_ready, c + 1)
                    if c >= 2:
                        act.wait_ge(h_ready, c - 1)
                    nc.scalar.activation(hn[c % 2][:, 0:k], ps[:, c % 2, 0:k], ACT.Relu).then_inc(hn_ready, 1)
                if 1 <= c < NCH + 1:
                    b = c - 1
                    k = P * len(tiles(b))
                    act.wait_ge(h_ready, b + 1)
                    if b >= 3:
                        act.wait_ge(rows_ready, b - 2)
                    nc.scalar.activation(ht[b % 3][:, 0:k], ps[:, 2, 0:k], ACT.Gelu, bias=b1_sb[:, :])\
                        .then_inc(ht_ready, 1)
                if 2 <= c < NCH + 2:
                    b = c - 2
                    k = P * len(tiles(b))
                    act.wait_ge(u_ready, b + 1)
                    if b >= 2:
                        act.wait_ge(own_ready, b - 1)
                    nc.scalar.activation(gu[b % 2][:, 0:k], ps[:, 3, 0:k], ACT.Gelu).then_inc(gu_ready, 1)
                    nc.scalar.activation(gh[b % 2][:, 0:k], ht[b % 3][:, 0:k], ACT.Gelu).then_inc(gh_ready, 1)
                if c >= 3:
                    h_rows(act, c - 3)
            act.wait_ge(ld_src, 16)
            act.wait_ge(marks_ready, 1)
            nc.scalar.activation(cf[:, MIX, :], iota_b[:, :], ACT.Copy, scale=0.0).then_inc(plane_set, 1)
            act.wait_ge(plane_set, 1)
            nc.scalar.activation(cf[:, MIX, MIX:PL], ring[:, 0, ROW:RS], ACT.Copy).then_inc(plane_set, 1)
            act.wait_ge(plane_set, 2)

            def split_step(i):
                for j in range(GPS):
                    index_copy(act, CT + U * i, i, j)
                    if j == 0:
                        act.wait_ge(crow_loaded, 16 * i)
                        act.wait_ge(rest_made, i)
                        for m in range(MIX):
                            nc.scalar.activation(cf[:, m, :], crow[:, 0:D], ACT.Copy, scale=crow[:, D + m:D + m + 1])
                        nc.scalar.activation(cf[:, MIX, 0:MIX], crow[:, D:ROW], ACT.Copy).then_inc(products_made, 1)
                    if j == 1:
                        act.wait_ge(products_made, i)
                        act.wait_ge(parts_free, i)
                        nc.scalar.activation(c3[:, :, 0, :], cf, ACT.Copy).then_inc(part_hi, 1)
                    if j == 5:
                        act.wait_ge(rest_made, i + 1)
                        nc.scalar.activation(c3[:, :, 1, :], rest, ACT.Copy).then_inc(part_mid, 1)

            for j in range(GPS):
                index_copy(act, CT, 0, j)
            with act.Fori(1, S1) as i:
                split_step(i)
            split_step(S1)
            with act.Fori(1, S2) as i:
                for j in range(GPS):
                    index_copy(act, CT + U * S1 + U * i, S1 + i, j)

            def index_step(eng, i, n):
                for j in range(GPS):
                    index_copy(eng, U * i, n, j)

            general_path(act, index_step)
            act.wait_ge(edges_done, 1)
            for c in range(NCH + AHEAD + 1):
                if c < NCH:
                    nc.scalar.activation(acc[:, 0:MIX, cols(c)], acc[:, 0:MIX, cols(c)], ACT.Gelu).then_inc(ga_ready, 1)
                if AHEAD <= c < NCH + AHEAD:
                    node_gelu(act, c - AHEAD)
                if c > AHEAD:
                    results(act, c - AHEAD - 1)

        @block.vector
        def _(v):
            link_count = [0]

            def link(ins):
                ins.then_inc(dve, 1)
                link_count[0] += 1

            def chained():
                v.wait_ge(dve, link_count[0])

            def statistics(a0, a1, part):
                v.wait_ge(ld_x[part], 16)
                for a in range(a0, a1):
                    link(nc.vector.bn_stats(stats[:, a, :], x_sb[:, a, :]))
                chained()
                for a in range(a0, a1):
                    link(nc.vector.bn_aggr(mv[:, a, :], stats[:, a, :]))
                chained()
                var, r = mv[:, a0:a1, 1], rstd[:, a0:a1]
                link(nc.vector.tensor_scalar_add(var, var, EPS))
                chained()
                link(nc.vector.tensor_scalar(r.bitcast(i32), var.bitcast(i32), 1, None, ALU.logical_shift_right))
                chained()
                link(nc.vector.tensor_scalar(r.bitcast(i32), r.bitcast(i32), -1.0, float(RSQRT_BITS),
                                             ALU.mult, ALU.add))
                for _ in range(3):
                    chained()
                    link(nc.vector.tensor_tensor(newton[:, a0:a1], r, r, ALU.mult))
                    chained()
                    link(nc.vector.scalar_tensor_tensor(newton[:, a0:a1], newton[:, a0:a1], -0.5, var,
                                                        ALU.mult, ALU.mult))
                    chained()
                    link(nc.vector.scalar_tensor_tensor(r, newton[:, a0:a1], 1.5, r, ALU.add, ALU.mult))
                chained()
                mean = mv[:, a0:a1, 0]
                nc.vector.scalar_tensor_tensor(mean, mean, -1.0, r, ALU.mult, ALU.mult).then_inc(stats_ready, 1)

            for q in (0, 1):
                statistics(XQ[q], XQ[q + 1], q)
            for c in range(NCH + 3):
                if c % 2 == 0 and c // 2 + 2 < XP:
                    q = c // 2 + 2
                    statistics(XQ[q], XQ[q + 1], q)
                if c == 1:
                    v.wait_ge(ld_dstg, 16)
                    nc.vector.tensor_reduce(gmin[:, :], dstg, axis=AX.X, op=ALU.min)
                    link(nc.vector.tensor_reduce(gmax[:, :], dstg, axis=AX.X, op=ALU.max))
                    chained()
                    nc.vector.tensor_tensor(gspan[:, :], gmax[:, :], gmin[:, :], ALU.subtract)\
                        .then_inc(bounds_ready, 1)
                if c >= 3:
                    table_rows(v, c - 3)
            v.wait_ge(ld_base, 32)
            v.wait_ge(ld_dst, 16)
            v.wait_ge(ld_src, 16)
            link(nc.vector.tensor_tensor(dloc.rearrange("p (g t) -> p g t", t=G),
                                         dst_i.rearrange("p (g t) -> p g t", t=G),
                                         base_b[:, :, None].to_broadcast([P, NG, G]), ALU.subtract))
            link(nc.vector.tensor_reduce(span[:, :], spans, axis=AX.X, op=ALU.max))
            link(nc.vector.tensor_reduce(marks[:, 0:1], spans, axis=AX.X, op=ALU.max))
            link(nc.vector.tensor_reduce(marks[:, 1:2], spans[:, 0:S1 * CG], axis=AX.X, op=ALU.max))
            link(nc.vector.tensor_tensor(tops, base_b[0:1, 0:S1 * CG], spans[:, 0:S1 * CG], ALU.add))
            link(nc.vector.tensor_scalar(key_a[:, :].bitcast(i32), src_i[:, 0:CT], P.bit_length() - 1, None,
                                         ALU.logical_shift_right))
            chained()
            link(nc.vector.tensor_reduce(marks[:, 2:3], tops, axis=AX.X, op=ALU.max))
            chained()
            link(nc.vector.tensor_copy(base, base_b[0:1, :]))
            nc.vector.tensor_scalar_min(base_c, base_b[0:1, 0:S1 * CG], float(CN)).then_inc(marks_ready, 1)
            link(nc.vector.scalar_tensor_tensor(key_b[:, :], key_a[:, :].bitcast(i32), -float(P), src_i[:, 0:CT],
                                                ALU.mult, ALU.add))
            link(nc.vector.scalar_tensor_tensor(key_a[:, :], key_a[:, :].bitcast(i32), float(CW), dloc[:, 0:CT],
                                                ALU.mult, ALU.add))
            link(nc.vector.memset(acc[:, MIX - 1, :], 0.0))
            v.wait_ge(own_stored[1], 16 * (NCH - EARLY))
            link(nc.vector.memset(words[:, 4 * EARLY * D:], 0.0))
            v.wait_ge(zeroed, NCH)
            v.wait_ge(marks_ready, 1)
            chained()
            with v.Fori(0, S1) as i:
                starts = window_starts(v, start_regs_c, base_c, CG * i, CN)

                def leave_rest():
                    v.wait_ge(part_hi, i + 1)
                    nc.vector.tensor_tensor(rest, cf, c3[:, :, 0, :], ALU.subtract).then_inc(rest_made, 1)

                def last_part():
                    v.wait_ge(part_mid, i + 1)
                    v.wait_ge(rest_made, i + 2)
                    nc.vector.tensor_tensor(c3[:, :, 2, :], rest, c3[:, :, 1, :], ALU.subtract).then_inc(part_lo, 1)

                scatter_step(v, CT + U * i, S1 * CG + GPS * i, i, {
                    0: lambda: hots(v, i, 0),
                    1: lambda: hots(v, i, 1),
                    2: lambda: (add_counts(v, i, 0, starts), hots(v, i, 2)),
                    4: lambda: (leave_rest(), add_counts(v, i, 1, starts), hots(v, i, 3)),
                    5: lambda: add_counts(v, i, 2, starts),
                    6: lambda: add_counts(v, i, 3, starts),
                })
                last_part()

            def product_steps(m0, m1):
                with v.Fori(m0, m1) as m:
                    with v.Fori(0, NAB) as ab:
                        u = NAB * m + ab
                        n = S1 + u
                        if m1 == 1:
                            nc.vector.tensor_reduce(most[:, bass.ds(ab, 1)], counts[:, bass.ds(AB * ab, AB), 0:CN],
                                                    axis=AX.XY, op=ALU.max).then_inc(most_made, 1)
                        scatter_step(v, CT + U * n, S1 * CG + GPS * n, n, {})
                        v.wait_ge(multiplied, u + 2)
                        v.wait_ge(added, GPS * (n + 1) + 1)
                        at = acc[:, bass.ds(m, 1), 0:CN].rearrange("p m n -> p (m n)")
                        nc.vector.tensor_tensor(at, at, ps[:, 5, 0:CN], ALU.add).then_inc(product_added, 1)
                        v.wait_ge(product_added, u + 2)
                        v.nop(nofuse=True)

            v.wait_ge(counts_added, S1 * CG + 1)
            product_steps(0, 1)
            v.wait_ge(most_made, NAB)
            nc.vector.tensor_reduce(most_p[:, :], most[:, :], axis=AX.X, op=ALU.max).then_inc(most_ready, 1)
            product_steps(1, PL)
            v.wait_ge(most_loaded, 16)
            link(nc.vector.tensor_reduce(marks[:, 3:4], most_r, axis=AX.X, op=ALU.max))
            chained()
            for q, least in enumerate((W, CW, CN, EXACT)):
                link(nc.vector.tensor_scalar(marks[:, q:q + 1], marks[:, q:q + 1], float(least), None, ALU.is_ge))
            chained()
            nc.vector.tensor_reduce(flag[:, :], marks[:, :], axis=AX.X, op=ALU.max).then_inc(flag_ready, 1)
            v.wait_ge(flag_ready, 1)
            flagged = v.value_load(flag[0:1, 0:1], min_val=0, max_val=1)
            with v.If(flagged >= 1):
                nc.vector.memset(acc[:, 0:MIX, :], 0.0).then_inc(cleared, 1)
                nc.vector.memset(accs, 0.0).then_inc(cleared, 1)
                v.wait_ge(cleared, 2)
                widest = v.value_load(span[0:1, 0:1], min_val=0, max_val=N)
                with v.Fori(0, PASSES) as q:
                    with v.If(widest >= q * W):
                        with v.Fori(0, STEPS) as i:
                            scatter_step(v, U * i, GPS * i, S1 + S2 + q * STEPS + i, {})
                        nc.vector.tensor_scalar(base, base, float(W), float(N), ALU.add, ALU.min).then_inc(moved, 1)
                        nc.vector.tensor_scalar_add(iota[:, :, :], iota[:, :, :], float(W)).then_inc(moved, 1)
                        v.wait_ge(moved, 2 * q + 2)
                        v.nop(nofuse=True)
            nc.vector.memset(done[:, :], 0.0).then_inc(edges_done, 1)
            v.wait_ge(sums_loaded, 16)
            count = sums_n[:, MIX, :]
            link(nc.vector.tensor_scalar_max(count, count, 1.0))
            chained()
            link(nc.vector.reciprocal(count, count))
            chained()
            link(nc.vector.tensor_tensor(weights_n, sums_n[:, 0:MIX, :],
                                         count[:, None, :].to_broadcast([P, MIX, NT]), ALU.mult))
            chained()
            link(nc.vector.tensor_copy(parts_n[:, :, 0, :], weights_n))
            chained()
            link(nc.vector.tensor_tensor(left_n, weights_n, parts_n[:, :, 0, :], ALU.subtract))
            chained()
            link(nc.vector.tensor_copy(parts_n[:, :, 1, :], left_n))
            chained()
            nc.vector.tensor_tensor(parts_n[:, :, 2, :], left_n, parts_n[:, :, 1, :], ALU.subtract)\
                .then_inc(weights_ready, 1)
            for c in range(NCH + 1):
                if c < NCH:
                    k = P * len(tiles(c))
                    v.wait_ge(ga_ready, c + 1)
                    for h in range(2):
                        t = 2 * c + h
                        v.wait_ge(spread, t + 1)
                        at = acc[:, 2 * h:2 * h + 2, cols(c)]
                        nc.vector.tensor_tensor(at, at, ps[:, 2 * (t % 3):2 * (t % 3) + 2, 0:k], ALU.mult)\
                            .then_inc(prod_ready, 1)
                if c >= 1:
                    v.wait_ge(pair_ready, c)
                    nc.vector.tensor_tensor(acc[:, 0, cols(c - 1)], acc[:, 0, cols(c - 1)], acc[:, 1, cols(c - 1)],
                                            ALU.add).then_inc(node_ready, 1)

        @block.tensor
        def _(pe):
            pe.wait_ge(consts, 7)
            pe.wait_ge(ld_w, 96)
            for c in range(NCH + 3):
                if c < NCH:
                    pe.wait_ge(z_ready, c + 1)
                    if c >= 2:
                        pe.wait_ge(hn_ready, c - 1)
                    for j in range(len(tiles(c))):
                        last = nc.tensor.transpose(ps[:, c % 2, P * j:P * j + P], z[c % 2][:, j, :], ident)
                    last.then_inc(zt_ready, 1)
                if 1 <= c < NCH + 1:
                    b = c - 1
                    k = P * len(tiles(b))
                    pe.wait_ge(hn_ready, b + 1)
                    if b >= 1:
                        pe.wait_ge(ht_ready, b)
                    nc.tensor.matmul(ps[:, 2, 0:k], w1_sb, hn[b % 2][:, 0:k], start=True, stop=True)\
                        .then_inc(h_ready, 1)
                if 2 <= c < NCH + 2:
                    b = c - 2
                    k = P * len(tiles(b))
                    pe.wait_ge(ht_ready, b + 1)
                    if b >= 1:
                        pe.wait_ge(gu_ready, b)
                    nc.tensor.matmul(ps[:, 3, 0:k], wa_sb, ht[b % 3][:, 0:k], start=True, stop=True)\
                        .then_inc(u_ready, 1)
                if c >= 3:
                    node_rows(pe, c - 3)
            for q in range(MS):
                last = nc.tensor.matmul(ps[:, q, MIX * W:PL * W], zero[:, :], zero[:, 0:W], start=True, stop=True)
            with pe.Fori(0, S1) as i:
                sum_step(pe, i, {1: lambda: count(pe, i, 0), 2: lambda: count(pe, i, 1),
                                 3: lambda: count(pe, i, 2), 5: lambda: count(pe, i, 3)})

            pe.wait_ge(counts_added, S1 * CG + 1)
            with pe.Fori(0, PL) as m:
                with pe.Fori(0, NAB) as ab:
                    u = NAB * m + ab

                    def multiply(a):
                        if a == 0:
                            pe.wait_ge(cbuf_loaded, 16 * u + 16)
                            pe.wait_ge(product_added, u + 1)
                        for part in range(SPL):
                            last = nc.tensor.matmul(
                                ps[:, 5, 0:CN], cbuf[:, a, part, :],
                                counts[:, bass.ds(AB * ab + a, 1), 0:CN].rearrange("p a n -> p (a n)"),
                                start=(a == 0 and part == 0), stop=(a == AB - 1 and part == SPL - 1))
                        if a == AB - 1:
                            last.then_inc(multiplied, 1)

                    sum_step(pe, S1 + u, {a: partial(multiply, a) for a in range(AB)})
            general_path(pe, lambda eng, i, n: sum_step(eng, n, {}))
            pe.wait_ge(weights_loaded, 16)
            pe.wait_ge(chosen, 5)
            pe.wait_ge(edges_done, 1)
            for c in range(NCH + 2):
                if c < NCH:
                    spread_weights(pe, c, 0)
                    spread_weights(pe, c, 1)
                if c >= 2:
                    project(pe, c - 2)


_OUT = "out_dram"


def kernel(x, src, dst, L0_gnn_W1, L0_gnn_b1, L0_gnn_WA, L0_gnn_WB, L0_gnn_W2, L0_gnn_b2):
    import numpy as _np
    import concourse.bacc as _bacc
    from concourse import mybir as _mybir
    from concourse.bass_utils import run_bass_kernel_spmd as _run

    def by_partition(a):
        return _np.ascontiguousarray(a.reshape(-1, P, *a.shape[1:]).swapaxes(0, 1))

    x, src, dst = _np.asarray(x), _np.asarray(src), _np.asarray(dst)
    w2 = _np.asarray(L0_gnn_W2)
    pad = ET * P - E
    laid_out = {
        "x": by_partition(_np.pad(x, ((0, NT * P - N), (0, 0)))),
        "src_by_edge": by_partition(_np.pad(src, (0, pad))),
        "dst_by_edge": by_partition(_np.pad(dst, (0, pad), constant_values=PAD_DST)),
        "dst_by_group": _np.pad(dst, (0, pad), mode="edge").reshape(GP, GC, G * P),
        "W1t": _np.asarray(L0_gnn_W1).T,
        "b1": _np.asarray(L0_gnn_b1).reshape(D, 1),
        "WAt": _np.asarray(L0_gnn_WA).T,
        "WBt": _np.asarray(L0_gnn_WB).T,
        "W2t": w2.T.reshape(2, D, D).swapaxes(0, 1),
        "b2": _np.asarray(L0_gnn_b2).reshape(1, D),
    }
    nc = _bacc.Bacc("TRN2", target_bir_lowering=False, num_devices=1)
    arrays, args = {}, []
    for name, a in laid_out.items():
        arrays[f"in_{name}"] = a = _np.ascontiguousarray(a)
        args.append(nc.dram_tensor(f"in_{name}", a.shape, _mybir.dt.from_np(a.dtype), kind="ExternalInput").ap())
    out = nc.dram_tensor(_OUT, (P, NT, D), _mybir.dt.float32, kind="ExternalOutput").ap()
    gnn_kernel(nc, *args, out)
    r = _run(nc, [arrays], core_ids=[0])
    return r.results[0][_OUT].swapaxes(0, 1).reshape(NT * P, D)[:N]
```
